# Optimizing a Trainium2 kernel written in Bass

```python
import numpy as np
import jax
import jax.numpy as jnp

def _softmax(x, axis=-1):
    return jax.nn.softmax(x, axis=axis)

def _gelu(x):
    return jax.nn.gelu(x, approximate=True)

def _silu(x):
    return jax.nn.silu(x)

def _sigmoid(x):
    return jax.nn.sigmoid(x)

def _layernorm(x, axis=-1, eps=1e-05):
    m = jnp.mean(x, axis=axis, keepdims=True)
    v = jnp.var(x, axis=axis, keepdims=True)
    return (x - m) / jnp.sqrt(v + eps)

def _scatter_add(tgt, idx, src, axis=0):
    return tgt.at[idx].add(src)

def _segment_sum(src, seg, n):
    return jax.ops.segment_sum(src, seg, n)
kernel_name = 'mk_prb_d1_jaxref_r4_ea2a1b'

def setup_inputs(seed: int=0):
    np.random.seed(seed)
    _w = jnp.asarray

    def _L0_attn_setup():
        import jax, jax.numpy as jnp
        import numpy as np
        N_STATE = 64
        SEQ_L = 1024
        BATCH, HCH = (16, 128)
        DT_MIN, DT_MAX = (0.001, 0.1)

        def _make_DPLR_HiPPO(N):
            P = np.sqrt(1 + 2 * np.arange(N))
            A = P[:, None] * P[None, :]
            A = np.tril(A) - np.diag(np.arange(N))
            nhippo = -A
            p = 0.5 * np.sqrt(2 * np.arange(1, N + 1) + 1.0)
            q = 2 * p
            S = nhippo + p[:, None] * q[None, :]
            Lambda, V = np.linalg.eig(S)
            Vc = V.conj().T
            p_t = Vc @ p
            q_t = Vc @ q.conj()
            return (Lambda, p_t, q_t, Vc)

        def _ri(z):
            return np.stack([z.real, z.imag], axis=-1).astype(np.float32)

        def _cplx(x_ri):
            return x_ri[..., 0] + 1j * x_ri[..., 1]

        def _s4_kernel(Lambda, p, q, B, Ct, step, L):
            Omega = jnp.exp(-2j * jnp.pi * (jnp.arange(L) / L))
            g = 2.0 / step * ((1.0 - Omega) / (1.0 + Omega))
            c = 2.0 / (1.0 + Omega)
            denom = g[:, None] - Lambda[None, :]
            cauchy = lambda v: (v[None, :] / denom).sum(-1)
            k00 = cauchy(Ct.conj() * B)
            k01 = cauchy(Ct.conj() * p)
            k10 = cauchy(q.conj() * B)
            k11 = cauchy(q.conj() * p)
            at_roots = c * (k00 - k01 * (1.0 / (1.0 + k11)) * k10)
            return jnp.fft.ifft(at_roots, L).real
        key = jax.random.key(seed)
        k_u, k_ct, k_b, k_d, k_ls = jax.random.split(key, 5)
        Lambda, p, q, Vc = _make_DPLR_HiPPO(N_STATE)
        u = jax.random.normal(k_u, (BATCH, HCH, SEQ_L), dtype=jnp.float32)
        Ct_ri = jax.random.normal(k_ct, (1, N_STATE, 2), dtype=jnp.float32) / np.sqrt(N_STATE)
        Bp = jax.random.normal(k_b, (N_STATE, 1), dtype=jnp.float32) / np.sqrt(N_STATE)
        D = jax.random.uniform(k_d, (1,), dtype=jnp.float32)
        log_step = jax.random.uniform(k_ls, (1,), dtype=jnp.float32, minval=np.log(DT_MIN), maxval=np.log(DT_MAX))
        return {'u': u, 'Lambda_ri': jnp.asarray(_ri(Lambda)), 'p_ri': jnp.asarray(_ri(p)), 'q_ri': jnp.asarray(_ri(q)), 'Vc_ri': jnp.asarray(_ri(Vc)), 'Ct_ri': Ct_ri, 'Bp': Bp, 'D': D, 'log_step': log_step}
    _L0_attn_in = _L0_attn_setup()

    def _L0_ffn_setup():
        import jax, jax.numpy as jnp
        import numpy as np
        GROUP = 64

        def dequantize(W_q, scale, zero):
            out, half = W_q.shape
            hi = W_q >> 4 & 15
            lo = W_q & 15
            w = jnp.stack([hi, lo], axis=-1).reshape(out, half * 2).astype(scale.dtype)
            w = w.reshape(out, -1, GROUP)
            w = (w - zero[:, :, None]) * scale[:, :, None]
            return w.reshape(out, half * 2)
        key = jax.random.key(seed)
        ks = jax.random.split(key, 10)
        hidden, inter = (1024, 2752)
        B, S = (4, 256)
        x = jax.random.normal(ks[0], (B, S, hidden), dtype=jnp.float32)
        gate_Wq = jax.random.randint(ks[1], (inter, hidden // 2), 0, 64, dtype=jnp.int32)
        up_Wq = jax.random.randint(ks[2], (inter, hidden // 2), 0, 64, dtype=jnp.int32)
        down_Wq = jax.random.randint(ks[3], (hidden, inter // 2), 0, 64, dtype=jnp.int32)
        gate_scale = jax.random.uniform(ks[4], (inter, hidden // GROUP)) * 0.01 + 0.0001
        gate_zero = jax.random.uniform(ks[5], (inter, hidden // GROUP)) * 15.0
        up_scale = jax.random.uniform(ks[6], (inter, hidden // GROUP)) * 0.01 + 0.0001
        up_zero = jax.random.uniform(ks[7], (inter, hidden // GROUP)) * 15.0
        down_scale = jax.random.uniform(ks[8], (hidden, inter // GROUP)) * 0.01 + 0.0001
        down_zero = jax.random.uniform(ks[9], (hidden, inter // GROUP)) * 15.0
        return {'x': x, 'gate_Wq': gate_Wq, 'up_Wq': up_Wq, 'down_Wq': down_Wq, 'gate_scale': gate_scale, 'gate_zero': gate_zero, 'up_scale': up_scale, 'up_zero': up_zero, 'down_scale': down_scale, 'down_zero': down_zero}
    _L0_ffn_in = _L0_ffn_setup()
    _d = {'L0_attn_u': _L0_attn_in['u'], 'L0_attn_Lambda_ri': _L0_attn_in['Lambda_ri'], 'L0_attn_p_ri': _L0_attn_in['p_ri'], 'L0_attn_q_ri': _L0_attn_in['q_ri'], 'L0_attn_Vc_ri': _L0_attn_in['Vc_ri'], 'L0_attn_Ct_ri': _L0_attn_in['Ct_ri'], 'L0_attn_Bp': _L0_attn_in['Bp'], 'L0_attn_D': _L0_attn_in['D'], 'L0_attn_log_step': _L0_attn_in['log_step'], 'L0_ffn_gate_Wq': _L0_ffn_in['gate_Wq'], 'L0_ffn_up_Wq': _L0_ffn_in['up_Wq'], 'L0_ffn_down_Wq': _L0_ffn_in['down_Wq'], 'L0_ffn_gate_scale': _L0_ffn_in['gate_scale'], 'L0_ffn_gate_zero': _L0_ffn_in['gate_zero'], 'L0_ffn_up_scale': _L0_ffn_in['up_scale'], 'L0_ffn_up_zero': _L0_ffn_in['up_zero'], 'L0_ffn_down_scale': _L0_ffn_in['down_scale'], 'L0_ffn_down_zero': _L0_ffn_in['down_zero']}
    _x0 = _d['L0_attn_u']
    _d['L0_attn_u'] = jax.random.normal(jax.random.fold_in(jax.random.key(seed), 1), (1, 2048, 1024), dtype=_x0.dtype)
    del _x0
    return _d

def reference(L0_attn_u, L0_attn_Lambda_ri, L0_attn_p_ri, L0_attn_q_ri, L0_attn_Vc_ri, L0_attn_Ct_ri, L0_attn_Bp, L0_attn_D, L0_attn_log_step, L0_ffn_gate_Wq, L0_ffn_up_Wq, L0_ffn_down_Wq, L0_ffn_gate_scale, L0_ffn_gate_zero, L0_ffn_up_scale, L0_ffn_up_zero, L0_ffn_down_scale, L0_ffn_down_zero):

    def _L0_attn_ref(u, Lambda_ri, p_ri, q_ri, Vc_ri, Ct_ri, Bp, D, log_step):
        import jax, jax.numpy as jnp
        import numpy as np
        N_STATE = 64
        SEQ_L = 1024
        BATCH, HCH = (16, 128)
        DT_MIN, DT_MAX = (0.001, 0.1)

        def _make_DPLR_HiPPO(N):
            P = np.sqrt(1 + 2 * np.arange(N))
            A = P[:, None] * P[None, :]
            A = np.tril(A) - np.diag(np.arange(N))
            nhippo = -A
            p = 0.5 * np.sqrt(2 * np.arange(1, N + 1) + 1.0)
            q = 2 * p
            S = nhippo + p[:, None] * q[None, :]
            Lambda, V = np.linalg.eig(S)
            Vc = V.conj().T
            p_t = Vc @ p
            q_t = Vc @ q.conj()
            return (Lambda, p_t, q_t, Vc)

        def _ri(z):
            return np.stack([z.real, z.imag], axis=-1).astype(np.float32)

        def _cplx(x_ri):
            return x_ri[..., 0] + 1j * x_ri[..., 1]

        def _s4_kernel(Lambda, p, q, B, Ct, step, L):
            Omega = jnp.exp(-2j * jnp.pi * (jnp.arange(L) / L))
            g = 2.0 / step * ((1.0 - Omega) / (1.0 + Omega))
            c = 2.0 / (1.0 + Omega)
            denom = g[:, None] - Lambda[None, :]
            cauchy = lambda v: (v[None, :] / denom).sum(-1)
            k00 = cauchy(Ct.conj() * B)
            k01 = cauchy(Ct.conj() * p)
            k10 = cauchy(q.conj() * B)
            k11 = cauchy(q.conj() * p)
            at_roots = c * (k00 - k01 * (1.0 / (1.0 + k11)) * k10)
            return jnp.fft.ifft(at_roots, L).real
        L = u.shape[-1]
        Lambda = _cplx(Lambda_ri)
        p = _cplx(p_ri)
        q = _cplx(q_ri)
        Vc = _cplx(Vc_ri)
        Ct = _cplx(Ct_ri).reshape(-1)
        B = (Vc @ Bp.astype(Vc.dtype)).reshape(-1)
        step = jnp.exp(log_step)[0]
        K = _s4_kernel(Lambda, p, q, B, Ct, step, L).astype(u.dtype)
        n = 2 * L
        y = jnp.fft.irfft(jnp.fft.rfft(u, n=n) * jnp.fft.rfft(K, n=n), n=n)[..., :L]
        return y + D[0] * u

    def _L0_ffn_ref(x, gate_Wq, up_Wq, down_Wq, gate_scale, gate_zero, up_scale, up_zero, down_scale, down_zero):
        import jax, jax.numpy as jnp
        import numpy as np
        GROUP = 64

        def dequantize(W_q, scale, zero):
            out, half = W_q.shape
            hi = W_q >> 4 & 15
            lo = W_q & 15
            w = jnp.stack([hi, lo], axis=-1).reshape(out, half * 2).astype(scale.dtype)
            w = w.reshape(out, -1, GROUP)
            w = (w - zero[:, :, None]) * scale[:, :, None]
            return w.reshape(out, half * 2)
        Wg = dequantize(gate_Wq, gate_scale, gate_zero)
        Wu = dequantize(up_Wq, up_scale, up_zero)
        Wd = dequantize(down_Wq, down_scale, down_zero)
        g = jnp.einsum('bsh,ih->bsi', x, Wg)
        u = jnp.einsum('bsh,ih->bsi', x, Wu)
        h = jax.nn.silu(g) * u
        return jnp.einsum('bsi,hi->bsh', h, Wd)
    x = L0_attn_u
    xn = _layernorm(x, axis=-1)
    x = x + _L0_attn_ref(xn, L0_attn_Lambda_ri, L0_attn_p_ri, L0_attn_q_ri, L0_attn_Vc_ri, L0_attn_Ct_ri, L0_attn_Bp, L0_attn_D, L0_attn_log_step) + _L0_ffn_ref(xn, L0_ffn_gate_Wq, L0_ffn_up_Wq, L0_ffn_down_Wq, L0_ffn_gate_scale, L0_ffn_gate_zero, L0_ffn_up_scale, L0_ffn_up_zero, L0_ffn_down_scale, L0_ffn_down_zero)
    return x

_drawn_inputs = setup_inputs


def setup_inputs(seed=0):
    import zlib

    import numpy as np

    out = dict(_drawn_inputs(seed))
    spreads = {}
    factors = {'L0_attn_Lambda_ri': 8.0,
     'L0_attn_p_ri': 8.0,
     'L0_attn_q_ri': 8.0,
     'L0_attn_Vc_ri': 8.0,
     'L0_attn_Ct_ri': 8.0,
     'L0_attn_Bp': 8.0}
    for name, (base, spread) in spreads.items():
        noise = np.random.default_rng([zlib.crc32(name.encode()), seed]).standard_normal(out[name].shape)
        drawn = base * np.exp(spread * noise) if base else spread * noise
        out[name] = jnp.asarray(drawn.astype(out[name].dtype))
    for name, factor in factors.items():
        out[name] = (out[name] * factor).astype(out[name].dtype)
    return out
```

```python
import numpy as np
import concourse.bass as bass
from concourse import mybir
from contextlib import ExitStack

S, H, I, NS = 2048, 1024, 2752, 64
P = 128
GROUP = 64
CH = 2 * P
NG = I // CH
TAIL = (I - NG * CH) // 2
SB = 512
NB = S // SB
KC = H // P
NT = S // P
SLAB = 512
L = H
M8 = L // P

XS, WS, KS = 2.0 ** 10, 2.0 ** 12, 2.0 ** 12
EPS = 1e-5


def s4_plus_int4_swiglu(nc, x_d, raw_gate, raw_up, raw_down, sz_gate, sz_up, sz_down,
                        tail_gate, tail_up, tail_down, tsz_gate, tsz_up, tsz_down,
                        lam_d, p_d, q_d, vc_d, ct_d, bp_d, d_d, ls_d,
                        ident_d, flip_d, angle_d, small_d, dft_d, twiddle_d, out_d):
    f32, f16, i32 = mybir.dt.float32, mybir.dt.float16, mybir.dt.int32
    ALU, ACT, AX = mybir.AluOpType, mybir.ActivationFunctionType, mybir.AxisListType

    ctx = ExitStack()
    with ctx:
        def sb(name, shape, dt=f32):
            return ctx.enter_context(nc.sbuf_tensor(name, shape, dt))

        def sem(name):
            return ctx.enter_context(nc.semaphore(name))

        acc = sb("acc", [P, NT, H])
        xh = sb("xh", [P, KC, S], f16)
        xl = sb("xl", [P, KC, S], f16)
        w_gu = [sb(f"w_gu{i}", [P, 2, 2, KC, CH], f16) for i in range(2)]
        w_dn = sb("w_dn", [P, 2, 2, H], f16)
        hh = sb("hh", [P, 2, 2, SB], f16)
        hl = sb("hl", [P, 2, 2, SB], f16)
        sil = sb("sil", [P, 2, SB])
        hf = sb("hf", [P, 2, SB])
        raw = sb("raw", [P, 2, SLAB], i32)
        sz = sb("sz", [P, 2, 2 * SLAB])
        wf = sb("wf", [P, 2, 2 * SLAB])
        ident = sb("ident", [P, P])
        stats = sb("stats", [P, 2, 2, 6])
        mv = sb("mv", [P, NT, 2])
        negm = sb("negm", [P, NT])
        vs = sb("vs", [P, NT])
        rstd = sb("rstd", [P, NT])
        half = sb("half", [P, 1])
        par = sb("par", [P, 5, 2])
        vcb = sb("vcb", [P, NS, 2])
        bpb = sb("bpb", [P, NS])
        vw = sb("vw", [P, 8])
        sc = sb("sc", [P, 8])
        d_sb = sb("d_sb", [1, 1])
        cs8 = sb("cs8", [P, 2, M8])
        e = sb("e", [P, 24, M8])
        kcol = sb("kcol", [P, M8])
        zrow = sb("zrow", [1, 2 * P])
        xn = w_gu[1][:, :, :, :, :].rearrange("p a b k c -> p (a b k c)").bitcast(f32)[:, 0:2 * H]\
            .rearrange("p (j h) -> p j h", j=2)
        s4w = w_gu[1][:, :, :, :, :].rearrange("p a b k c -> p (a b k c)").bitcast(f32)\
            .rearrange("p (j h) -> p j h", j=4)
        strip = w_gu[1][:, 0, :, :, :].rearrange("p b k c -> p b (k c)")\
            .rearrange("p b (n t) -> p b n t", n=2)
        angle = sz
        kshift = wf
        dft = raw[:, 0, 0:2 * P].bitcast(f32).rearrange("p (j a) -> p j a", j=2)
        flip = raw[:, 0, 2 * P:3 * P].bitcast(f32)
        twiddle = raw[:, 1, 0:P].bitcast(f32)
        krow = raw[0:M8, 1, P:2 * P].bitcast(f32)

        pg = [ctx.enter_context(nc.psum_tensor(f"pg{i}", [P, SB], f32)) for i in range(2)]
        pu = [ctx.enter_context(nc.psum_tensor(f"pu{i}", [P, SB], f32)) for i in range(2)]
        po = [ctx.enter_context(nc.psum_tensor(f"po{i}", [P, SB], f32)) for i in range(4)]

        kpad = nc.dram_tensor("kpad", [CH + L], f32, kind="Internal").ap()

        x_in = [sem(f"x_in{j}") for j in range(NT)]
        slab_in = [sem(f"slab_in{j}") for j in range(2)]
        ident_in, par_in, tab_in, kpad_out, kshift_in, out_done = \
            (sem(n) for n in ("ident_in", "par_in", "tab_in", "kpad_out", "kshift_in", "out_done"))
        consts, stat_done, rstd_done, xn_done, xt_done, xhi_done, xlo_done = \
            (sem(n) for n in ("consts", "stat_done", "rstd_done", "xn_done", "xt_done", "xhi_done", "xlo_done"))
        gate_done, up_done, down_done, silu_done, hf_done, hhi_done, hlo_done, acc_done = \
            (sem(n) for n in ("gate_done", "up_done", "down_done", "silu_done", "hf_done", "hhi_done",
                              "hlo_done", "acc_done"))
        wprep_done, whi_done, wlo_done, dve_order = \
            (sem(n) for n in ("wprep_done", "whi_done", "wlo_done", "dve_order"))
        dve_order_loop = sem("dve_order_loop")
        step_done, cauchy_done, s4_read, dft_done, krow_done, kzero_done, kt_done = \
            (sem(n) for n in ("step_done", "cauchy_done", "s4_read", "dft_done", "krow_done",
                              "kzero_done", "kt_done"))
        resolvent_done, roots_done, kcol_done, flip_done, shi_done, slo_done = \
            (sem(n) for n in ("resolvent_done", "roots_done", "kcol_done", "flip_done", "shi_done", "slo_done"))
        conv_done, conv_added, pool_order = (sem(n) for n in ("conv_done", "conv_added", "pool_order"))

        def rows(tail):
            return TAIL if tail else P

        def words(k, tail):
            return 2 * (2 * TAIL) if tail and k < 4 else SLAB

        def raw_view(slot, k, tail):
            n = rows(tail) if k >= 4 else P
            return raw[0:n, slot, 0:words(k, tail)]

        def sz_view(slot, k, tail):
            n = rows(tail) if k >= 4 else P
            w = words(k, tail)
            if k >= 4:
                v = sz[0:n, slot, 0:2 * w].rearrange("p (z w) -> p z w", z=2)
                return [v[:, z:z + 1, :].broadcast_to((n, 2, w)) for z in range(2)]
            v = sz[0:n, slot, 0:2 * w].rearrange("p (c z w) -> p c z w", c=2, z=2)
            return [v[:, None, :, z, :].broadcast_to((n, 2, 2, w // 2)) for z in range(2)]

        def wf_view(slot, k, tail, dt=f32):
            n = rows(tail) if k >= 4 else P
            w = words(k, tail)
            v = wf[0:n, slot, 0:2 * w]
            v = v.bitcast(dt) if dt != f32 else v
            if k >= 4:
                return v.rearrange("p (a w) -> p a w", a=2)
            return v.rearrange("p (a c w) -> p a c w", a=2, c=2)

        def w_flat(slot, k, tail):
            n = rows(tail) if k >= 4 else P
            w = words(k, tail)
            if k >= 4:
                return wf[0:n, slot, 0:2 * w].rearrange("p (a w) -> p a w", a=2)
            return wf[0:n, slot, 0:2 * w].rearrange("p (c w) -> p c w", c=4)

        def w_dest(parity, k, part, tail):
            if k >= 4:
                return w_dn[0:rows(tail), part, :, (k - 4) * SLAB:(k - 3) * SLAB]
            return w_gu[parity][:, k // 2, part, 4 * (k % 2):4 * (k % 2) + 4, 0:2 * rows(tail)]

        X_LATER = (range(4, 8), range(8, NT))
        LOOP = (1, NG - 1)

        block = ctx.enter_context(nc.Block())

        @block.sync
        def _(sp):
            def load_slab(g, k, tail=False, free=True):
                slot = k % 2
                if free:
                    sp.wait_ge(wprep_done, 6 * g + k - 1)
                n = rows(tail) if k >= 4 else P
                w = words(k, tail)
                q = (n + 31) // 32
                if tail:
                    r = (tail_gate, tail_up, tail_down)[k // 2]
                    z = (tsz_gate, tsz_up, tsz_down)[k // 2]
                    r = r[:, (k % 2) * w:(k % 2 + 1) * w]
                    z = z[:, (k % 2) * 2 * w:(k % 2 + 1) * 2 * w]
                else:
                    r = (raw_gate, raw_up, raw_down)[k // 2]
                    z = (sz_gate, sz_up, sz_down)[k // 2]
                    r = r[bass.ds(g, 1), :, (k % 2) * w:(k % 2 + 1) * w].rearrange("g p w -> (g p) w")
                    z = z[bass.ds(g, 1), :, (k % 2) * 2 * w:(k % 2 + 1) * 2 * w].rearrange("g q w -> (g q) w")
                sp.dma_start(raw[0:n, slot, 0:w], r).then_inc(slab_in[slot], 16)
                sp.dma_start(sz[0:n, slot, 0:2 * w], z[:, None, :].broadcast_to((q, 32, 2 * w)))\
                    .then_inc(slab_in[slot], 16)

            for k in range(6):
                load_slab(0, k, free=k >= 2)
            for k in range(6):
                load_slab(1, k)
            with sp.Fori(0, (LOOP[1] - LOOP[0]) // 2) as it:
                for half_turn in range(2):
                    for k in range(6):
                        load_slab(2 * it + (LOOP[0] + half_turn + 1), k)
            for k in range(6):
                load_slab(NG, k, tail=True)
            sp.wait_ge(wprep_done, 6 * NG + 6)
            for j in range(2):
                sp.dma_start(angle[:, j, :], angle_d[j:j + 1, :].broadcast_to((P, L))).then_inc(tab_in, 16)
            sp.dma_start(dft, dft_d).then_inc(tab_in, 16)
            sp.dma_start(flip, flip_d).then_inc(tab_in, 16)
            sp.dma_start(twiddle, twiddle_d).then_inc(tab_in, 16)
            sp.dma_start(cs8[:, :, :], small_d).then_inc(tab_in, 16)
            sp.wait_ge(kzero_done, 1)
            sp.dma_start(kpad[0:CH][None, :], zrow[0:1, :]).then_inc(kpad_out, 16)
            sp.wait_ge(krow_done, 1)
            sp.dma_start(kpad[CH:CH + L].rearrange("(b a) -> b a", b=M8), krow).then_inc(kpad_out, 16)
            sp.wait_ge(kpad_out, 32)
            for n in range(2):
                src = bass.AP(kpad.tensor, 2 - n, [[2, P], [1, L]])
                sp.dma_start(kshift[:, n, :], src).then_inc(kshift_in, 16)
            for st in range(NT):
                sp.wait_ge(conv_added, 2 * st + 2)
                sp.dma_start(out_d[st * P:(st + 1) * P, :], acc[:, st, :]).then_inc(out_done, 16)
            sp.wait_ge(out_done, 16 * NT)

        @block.gpsimd
        def _(pool):
            pool.memset(half[:, :], -0.5).then_inc(pool_order, 1)
            pool.memset(zrow[:, :], 0.0).then_inc(kzero_done, 1)
            pool.memset(sc[:, 7:8], float(np.e)).then_inc(pool_order, 1)
            pool.wait_ge(pool_order, 2)

            def normalize(j):
                pool.wait_ge(stat_done, j + 1)
                pool.tensor_tensor(rstd[:, j:j + 1], vs[:, j:j + 1], half[:, :], ALU.pow).then_inc(rstd_done, 1)
                pool.wait_ge(rstd_done, j + 1)
                if j >= 2:
                    pool.wait_ge(xt_done, 2 * j - 2)
                pool.tensor_scalar(xn[:, j % 2, :], acc[:, j, :], negm[:, j:j + 1], rstd[:, j:j + 1],
                                   ALU.add, ALU.mult).then_inc(xn_done, 1)

            def w_low(g, k, parity, tail=False):
                pool.wait_ge(whi_done, 6 * g + k + 1)
                pool.tensor_tensor(w_dest(parity, k, 1, tail), w_flat(k % 2, k, tail), w_dest(parity, k, 0, tail),
                                   ALU.subtract).then_inc(wlo_done, 1)

            def h_low(g, b, t, tail=False):
                n = rows(tail)
                pool.wait_ge(hhi_done, 8 * g + 2 * b + t + 1)
                pool.tensor_tensor(hl[0:n, b % 2, t, :], hf[0:n, t, :], hh[0:n, b % 2, t, :],
                                   ALU.subtract).then_inc(hlo_done, 1)

            def group(g, parity, first=False, tail=False, next_tail=False):
                for b in range(NB):
                    if first and b < 2:
                        for j in X_LATER[b]:
                            normalize(j)
                    h_low(g, b, 0, tail)
                    if not tail:
                        if b == 1:
                            w_low(g + 1, 0, 1 - parity, next_tail)
                        if b == 3:
                            w_low(g + 1, 3, 1 - parity, next_tail)
                    h_low(g, b, 1, tail)
                    if not tail and b == 2:
                        w_low(g + 1, 1, 1 - parity, next_tail)
                        w_low(g + 1, 2, 1 - parity, next_tail)
                    if b == 0:
                        w_low(g, 4, parity, tail)
                        w_low(g, 5, parity, tail)

            for k in range(2):
                w_low(0, k, 0)
            for j in range(4):
                normalize(j)
            for k in range(2, 4):
                w_low(0, k, 0)
            group(0, 0, first=True)
            pool.wait_ge(par_in, 16 * 13)
            pool.tensor_tensor(sc[:, 1:2], sc[:, 7:8], sc[:, 0:1], ALU.pow).then_inc(step_done, 1)
            with pool.Fori(0, (LOOP[1] - LOOP[0]) // 2) as it:
                for half_turn in range(2):
                    group(2 * it + (LOOP[0] + half_turn), (LOOP[0] + half_turn) % 2)
            group(NG - 1, (NG - 1) % 2, next_tail=True)
            group(NG, NG % 2, tail=True)

        @block.scalar
        def _(act):
            act.dma_start(ident[:, :], ident_d).then_inc(ident_in, 16)
            for j in range(NT):
                act.dma_start(acc[:, j, :], x_d[j * P:(j + 1) * P, :]).then_inc(x_in[j], 16)
            for h2 in range(2):
                for i, src in enumerate((lam_d, p_d, q_d, ct_d)):
                    act.dma_start(par[h2 * NS:(h2 + 1) * NS, i, :], src).then_inc(par_in, 16)
                act.dma_start(vcb[h2 * NS:(h2 + 1) * NS, :, :], vc_d).then_inc(par_in, 16)
            act.dma_start(bpb[:, :], bp_d.rearrange("n a -> a n").broadcast_to((P, NS))).then_inc(par_in, 16)
            act.dma_start(sc[:, 0:1], ls_d[:, None].broadcast_to((P, 1))).then_inc(par_in, 16)
            act.dma_start(d_sb[:, :], d_d[:, None]).then_inc(par_in, 16)

            def x_high(j):
                for hf2 in range(2):
                    act.wait_ge(xt_done, 2 * j + hf2 + 1)
                    act.activation(xh[:, 4 * hf2:4 * hf2 + 4, j * P:(j + 1) * P],
                                   po[2 * (j % 2) + hf2][:, :].rearrange("p (k s) -> p k s", k=4),
                                   ACT.Copy).then_inc(xhi_done, 1)

            def w_high(g, k, parity, tail=False, first=False):
                act.wait_ge(wprep_done, 6 * g + k + 1)
                if not first:
                    if k < 4:
                        act.wait_ge(up_done, 8 * g - 8)
                    else:
                        act.wait_ge(down_done, 32 * g)
                act.activation(w_dest(parity, k, 0, tail), w_flat(k % 2, k, tail), ACT.Copy)\
                    .then_inc(whi_done, 1)

            def silu(g, b, t, first, tail):
                n = rows(tail)
                idx = 8 * g + 2 * b + t
                act.wait_ge(gate_done, idx + 1)
                if not (first and b == 0):
                    act.wait_ge(hf_done, idx - 1)
                act.activation(sil[0:n, t, :], pg[t][0:n, :], ACT.Silu, scale=1.0 / (XS * WS))\
                    .then_inc(silu_done, 1)

            def h_high(g, b, t, first, tail):
                n = rows(tail)
                act.wait_ge(hf_done, 8 * g + 2 * b + t + 1)
                if not (first and b < 2):
                    act.wait_ge(down_done, 32 * g + 8 * b - 8)
                act.activation(hh[0:n, b % 2, t, :], hf[0:n, t, :], ACT.Copy).then_inc(hhi_done, 1)

            def group(g, parity, first=False, tail=False, next_tail=False):
                for b in range(NB):
                    if first and b < 2:
                        for j in X_LATER[b]:
                            x_high(j)
                    silu(g, b, 0, first, tail)
                    h_high(g, b, 0, first, tail)
                    if not tail:
                        if b == 1:
                            if first:
                                act.wait_ge(xt_done, 2 * NT)
                            w_high(g + 1, 0, 1 - parity, next_tail)
                        if b == 3:
                            w_high(g + 1, 3, 1 - parity, next_tail)
                    silu(g, b, 1, first, tail)
                    h_high(g, b, 1, first, tail)
                    if not tail and b == 2:
                        w_high(g + 1, 1, 1 - parity, next_tail)
                        w_high(g + 1, 2, 1 - parity, next_tail)
                    if b == 0:
                        w_high(g, 4, parity, tail, first)
                        w_high(g, 5, parity, tail, first)

            for k in range(2):
                w_high(0, k, 0, first=True)
            for j in range(4):
                x_high(j)
            for k in range(2, 4):
                w_high(0, k, 0, first=True)
            group(0, 0, first=True)
            with act.Fori(0, (LOOP[1] - LOOP[0]) // 2) as it:
                for half_turn in range(2):
                    group(2 * it + (LOOP[0] + half_turn), (LOOP[0] + half_turn) % 2)
            group(NG - 1, (NG - 1) % 2, next_tail=True)
            group(NG, NG % 2, tail=True)
            for n in range(2):
                for c in range(2):
                    act.wait_ge(flip_done, 2 * n + c + 1)
                    act.activation(strip[:, 0, n, c * SB:(c + 1) * SB], (pg, pu)[n][c][:, :], ACT.Copy,
                                   scale=KS).then_inc(shi_done, 1)

        @block.tensor
        def _(pe):
            pe.wait_ge(ident_in, 16)

            def x_transpose(j):
                pe.wait_ge(xn_done, j + 1)
                for hf2 in range(2):
                    if j >= 2:
                        pe.wait_ge(xlo_done, 2 * j + hf2 - 3)
                    for kk in range(4):
                        first_h = 2 * P * (2 * hf2 + kk % 2) + kk // 2
                        last = pe.transpose(po[2 * (j % 2) + hf2][:, kk * P:(kk + 1) * P],
                                            xn[:, j % 2, first_h:first_h + 2 * P - 1:2], ident[:, :])
                    last.then_inc(xt_done, 1)

            def project(g, b, t, mat, parity, first, tail):
                n = rows(tail)
                idx = 8 * g + 2 * b + t
                bank = (pg, pu)[mat][t]
                if not (first and b == 0):
                    pe.wait_ge((silu_done, hf_done)[mat], idx - 1)
                w = w_gu[parity]
                toks = slice(b * SB, (b + 1) * SB)
                for k in range(KC):
                    for wp, xp in ((0, xh), (0, xl), (1, xh)):
                        last = pe.matmul(bank[0:n, :], w[:, mat, wp, k, t * n:(t + 1) * n], xp[:, k, toks],
                                         start=(k == 0 and wp == 0 and xp is xh), stop=(k == KC - 1 and wp == 1))
                last.then_inc((gate_done, up_done)[mat], 1)

            def down(g, b, tail=False, first=False):
                n = rows(tail)
                pe.wait_ge(hlo_done, 8 * g + 2 * b + 2)
                for d in range(8):
                    st, hd = d // 2, d % 2
                    if not (first and b == 0 and d < 4):
                        pe.wait_ge(acc_done, 32 * g + 8 * b + d - 3)
                    for t in range(2):
                        for hp, wp in ((hh, 0), (hh, 1), (hl, 0)):
                            last = pe.matmul(po[d % 4][:, :], hp[0:n, b % 2, t, st * P:(st + 1) * P],
                                             w_dn[0:n, wp, t, hd * SB:(hd + 1) * SB],
                                             start=(t == 0 and wp == 0 and hp is hh),
                                             stop=(t == 1 and hp is hl))
                    last.then_inc(down_done, 1)

            def group(g, parity, first=False, tail=False, between=None):
                for b in range(NB):
                    if first:
                        pe.wait_ge(xlo_done, 8 * b + 8)
                    for t in range(2):
                        for mat in range(2):
                            if b == 0 and t == 0:
                                pe.wait_ge(wlo_done, 6 * g + 2 + 2 * mat)
                            if tail and b >= 2 and t == 0 and mat == 0:
                                pe.wait_ge(s4_read, b - 1)
                            project(g, b, t, mat, parity, first, tail)
                    if first and b < 2:
                        for j in X_LATER[b]:
                            x_transpose(j)
                    if between:
                        between(b)
                    if b == 0 and not first:
                        down(g - 1, NB - 1)
                    if b == 1:
                        pe.wait_ge(wlo_done, 6 * g + 6)
                        if first:
                            pe.wait_ge(xlo_done, 2 * NT)
                    if b >= 1:
                        down(g, b - 1, tail, first)

            def s4_steps(b):
                if b == 1:
                    pe.wait_ge(resolvent_done, 1)
                    pe.wait_ge(silu_done, 8 * NG + 3)
                    for m in range(M8):
                        last = pe.matmul(pg[0][:, 8 * m:8 * m + 8], s4w[:, 2, m:L:M8], vw[:, :],
                                         start=True, stop=True)
                    last.then_inc(cauchy_done, 1)
                if b == 2:
                    pe.wait_ge(roots_done, 1)
                    pe.wait_ge(silu_done, 8 * NG + 5)
                    pe.matmul(pg[0][:, 0:2 * M8], dft[:, 0, :], e[:, 1:3, :], start=True, stop=False)
                    pe.matmul(pg[0][:, 0:2 * M8], dft[:, 1, :], e[:, 0:2, :], start=False, stop=True)\
                        .then_inc(dft_done, 1)
                if b == 3:
                    pe.wait_ge(kcol_done, 1)
                    pe.wait_ge(silu_done, 8 * NG + 7)
                    pe.transpose(pg[0][0:M8, 0:P], kcol[:, :], ident[:, :]).then_inc(kt_done, 1)

            for j in range(4):
                x_transpose(j)
            group(0, 0, first=True)
            with pe.Fori(0, (LOOP[1] - LOOP[0]) // 2) as it:
                for half_turn in range(2):
                    group(2 * it + (LOOP[0] + half_turn), (LOOP[0] + half_turn) % 2)
            group(NG - 1, (NG - 1) % 2)
            group(NG, NG % 2, tail=True, between=s4_steps)
            pe.wait_ge(kshift_in, 32)
            pe.wait_ge(hf_done, 8 * NG + 8)
            pe.wait_ge(krow_done, 1)
            for n in range(2):
                for c in range(2):
                    pe.matmul((pg, pu)[n][c][:, :], flip, kshift[:, n, c * SB:(c + 1) * SB],
                              start=True, stop=True).then_inc(flip_done, 1)
            down(NG, NB - 1, True)
            pe.wait_ge(slo_done, 4)
            for st in range(NT):
                for c in range(2):
                    d = 2 * st + c
                    pe.wait_ge(acc_done, 32 * (NG + 1) - 3 + min(d, 3))
                    if d >= 4:
                        pe.wait_ge(conv_added, d - 3)
                    chunks = [k for k in range(KC) if 2 * P * (2 * (k // 4) + k % 2) < (c + 1) * SB]
                    for k in chunks:
                        h0, nib = 2 * P * (2 * (k // 4) + k % 2), (k // 2) % 2
                        t0 = max(c * SB, h0)
                        for xp, sp_ in ((xh, 0), (xh, 1), (xl, 0)):
                            last = pe.matmul(po[d % 4][:, t0 - c * SB:SB], xp[:, k, st * P:(st + 1) * P],
                                             strip[:, sp_, nib, t0 - h0:(c + 1) * SB - h0],
                                             start=(k == 0 and xp is xh and sp_ == 0),
                                             stop=(k == chunks[-1] and xp is xl))
                    last.then_inc(conv_done, 1)

        @block.vector
        def _(dve):
            chain = [0]

            def link(ins):
                chain[0] += 1
                ins.then_inc(dve_order, 1)
                dve.wait_ge(dve_order, chain[0])

            def x_stats(j):
                dve.wait_ge(x_in[j], 16)
                for c in range(2):
                    last = dve.bn_stats(stats[:, j % 2, c, :], acc[:, j, c * SB:(c + 1) * SB])
                link(last)
                link(dve.bn_aggr(mv[:, j, :], stats[:, j % 2, :, :].rearrange("p c s -> p (c s)")))
                link(dve.tensor_scalar(negm[:, j:j + 1], mv[:, j, 0:1], -1.0, None, ALU.mult))
                dve.tensor_scalar(vs[:, j:j + 1], mv[:, j, 1:2], XS ** -2, EPS * XS ** -2, ALU.mult, ALU.add)\
                    .then_inc(stat_done, 1)

            def x_low(j):
                for hf2 in range(2):
                    dst = (slice(None), slice(4 * hf2, 4 * hf2 + 4), slice(j * P, (j + 1) * P))
                    dve.wait_ge(xhi_done, 2 * j + hf2 + 1)
                    dve.tensor_tensor(xl[dst], po[2 * (j % 2) + hf2][:, :].rearrange("p (k s) -> p k s", k=4),
                                      xh[dst], ALU.subtract).then_inc(xlo_done, 1)

            def w_prep(g, k, tail=False, free=True):
                slot, n = k % 2, 6 * g + k
                dve.wait_ge(slab_in[slot], 32 * 3 * g + 32 * (k // 2 + 1))
                if free:
                    dve.wait_ge(wlo_done, n - 1)
                q = wf_view(slot, k, tail, i32)
                w = wf_view(slot, k, tail)
                r = raw_view(slot, k, tail)
                if k < 4:
                    r = r.rearrange("p (c w) -> p c w", c=2)
                scale, zero = sz_view(slot, k, tail)
                dve.tensor_scalar(q[:, 0], r, 4, 15, ALU.arith_shift_right, ALU.bitwise_and)
                dve.tensor_scalar(q[:, 1], r, 15, None, ALU.bitwise_and).then_inc(dve_order_loop, 1)
                dve.wait_ge(dve_order_loop, 2 * n + 1)
                dve.tensor_tensor(w, q, zero, ALU.subtract).then_inc(dve_order_loop, 1)
                dve.wait_ge(dve_order_loop, 2 * n + 2)
                for nib in range(2):
                    last = dve.scalar_tensor_tensor(out=w[:, nib], in0=w[:, nib], scalar=WS, in1=scale[:, nib],
                                                    op0=ALU.mult, op1=ALU.mult)
                last.then_inc(wprep_done, 1)

            def h_mult(g, b, t, first, tail):
                n = rows(tail)
                idx = 8 * g + 2 * b + t
                dve.wait_ge(up_done, idx + 1)
                dve.wait_ge(silu_done, idx + 1)
                if not (first and b == 0):
                    dve.wait_ge(hlo_done, idx - 1)
                dve.scalar_tensor_tensor(out=hf[0:n, t, :], in0=pu[t][0:n, :], scalar=1.0 / (XS * WS),
                                         in1=sil[0:n, t, :], op0=ALU.mult, op1=ALU.mult).then_inc(hf_done, 1)

            def accumulate(g, b):
                for d in range(8):
                    part = acc[:, 4 * b + d // 2, (d % 2) * SB:(d % 2 + 1) * SB]
                    dve.wait_ge(down_done, 32 * g + 8 * b + d + 1)
                    dve.scalar_tensor_tensor(out=part, in0=po[d % 4][:, :], scalar=1.0 / WS, in1=part,
                                             op0=ALU.mult, op1=ALU.add).then_inc(acc_done, 1)

            def resolvent():
                dve.wait_ge(par_in, 16 * 13)
                dve.wait_ge(step_done, 1)
                dve.wait_ge(tab_in, 16 * 6)
                t3 = e[:, 0:16, :].rearrange("p a m -> p (a m)").rearrange("p (r n) -> p r n", r=2)
                link(dve.tensor_tensor(t3, vcb[:, :, :].rearrange("p n r -> p r n"),
                                       bpb[:, None, :].broadcast_to((P, 2, NS)), ALU.mult))
                link(dve.tensor_reduce(par[:, 4, :], t3, AX.X, ALU.add))
                ar = e[:, 16, 0:2]
                ai = e[:, 16, 2:4]
                br = e[:, 16, 4:6]
                bi = e[:, 16, 6:8]
                for dst, src in ((ar, (3, 2)), (br, (4, 1))):
                    for j in range(2):
                        dve.tensor_copy(dst[:, j:j + 1], par[:, src[j], 0:1])
                for dst, src in ((ai, (3, 2)), (bi, (4, 1))):
                    for j in range(2):
                        last = dve.tensor_copy(dst[:, j:j + 1], par[:, src[j], 1:2])
                link(last)

                def outer(a, b_):
                    return a[:, :, None].broadcast_to((P, 2, 2)), b_[:, None, :].broadcast_to((P, 2, 2))

                m = [e[:, 17 + j // 2, 4 * (j % 2):4 * (j % 2) + 4].rearrange("p (a b) -> p a b", a=2)
                     for j in range(4)]
                for o, (a, b_) in zip(m, ((ar, br), (ai, bi), (ar, bi), (ai, br))):
                    i0, i1 = outer(a, b_)
                    last = dve.tensor_tensor(o, i0, i1, ALU.mult)
                link(last)
                v = [e[:, 19, 4 * j:4 * j + 4].rearrange("p (a b) -> p a b", a=2) for j in range(2)]
                dve.tensor_tensor(v[0], m[0], m[1], ALU.add)
                link(dve.tensor_tensor(v[1], m[2], m[3], ALU.subtract))
                dve.tensor_copy(vw[0:NS, :], e[0:NS, 19, :])
                dve.tensor_scalar(vw[NS:P, 0:4], e[NS:P, 19, 4:8], -1.0, None, ALU.mult)
                dve.tensor_copy(vw[NS:P, 4:8], e[NS:P, 19, 0:4])
                link(dve.reciprocal(sc[:, 2:3], sc[:, 1:2]))
                link(dve.tensor_scalar(sc[:, 2:3], sc[:, 2:3], 2.0, None, ALU.mult))
                dve.tensor_scalar(sc[:, 3:5], par[:, 0, :], -1.0, None, ALU.mult)
                dve.tensor_scalar(sc[0:NS, 5:6], par[0:NS, 0, 0:1], -1.0, None, ALU.mult)
                dve.tensor_copy(sc[NS:P, 5:6], par[NS:P, 0, 1:2])
                dve.memset(sc[0:NS, 6:7], 0.0)
                link(dve.tensor_scalar(sc[NS:P, 6:7], sc[NS:P, 2:3], -1.0, None, ALU.mult))
                dve.wait_ge(up_done, 8 * NG)
                re, im, res = s4w[:, 0, :], s4w[:, 1, :], s4w[:, 2, :]
                dve.tensor_scalar(re, angle[:, 0, :], sc[:, 3:4], None, ALU.mult)
                dve.tensor_scalar(im, angle[:, 1, :], sc[:, 2:3], None, ALU.mult)
                link(dve.tensor_scalar(res, angle[:, 0, :], sc[:, 5:6], None, ALU.mult))
                dve.scalar_tensor_tensor(out=im, in0=angle[:, 0, :], scalar=sc[:, 4:5], in1=im,
                                         op0=ALU.mult, op1=ALU.add)
                link(dve.scalar_tensor_tensor(out=res, in0=angle[:, 1, :], scalar=sc[:, 6:7], in1=res,
                                              op0=ALU.mult, op1=ALU.add))
                dve.tensor_tensor(re, re, re, ALU.mult)
                link(dve.tensor_tensor(im, im, im, ALU.mult))
                link(dve.tensor_tensor(re, re, im, ALU.add))
                link(dve.reciprocal(re, re))
                dve.tensor_tensor(res, res, re, ALU.mult).then_inc(resolvent_done, 1)

            def cauchy_sums():
                dve.wait_ge(cauchy_done, 1)
                sums = pg[0][:, 0:8 * M8].rearrange("p (m j) -> p j m", j=8)
                dve.tensor_copy(e[:, 3:11, :], sums).then_inc(s4_read, 1)

            def roots():
                dve.wait_ge(s4_read, 1)
                r00, r01, r10, r11, i00, i01, i10, i11 = (e[:, 3 + j, :] for j in range(8))
                co, si = cs8[:, 0, :], cs8[:, 1, :]
                t = [e[:, 11 + j, :] for j in range(13)]
                mul, add, sub = ALU.mult, ALU.add, ALU.subtract
                dve.tensor_tensor(t[0], r01, r10, mul)
                dve.tensor_tensor(t[1], i01, i10, mul)
                dve.tensor_tensor(t[2], r01, i10, mul)
                dve.tensor_tensor(t[3], i01, r10, mul)
                dve.tensor_tensor(t[4], co, r11, mul)
                link(dve.tensor_tensor(t[5], co, i11, mul))
                dve.tensor_tensor(t[0], t[0], t[1], sub)
                dve.tensor_tensor(t[2], t[2], t[3], add)
                link(dve.tensor_scalar(t[4], t[4], 1.0, None, add))
                dve.tensor_tensor(t[6], t[4], t[4], mul)
                link(dve.tensor_tensor(t[7], t[5], t[5], mul))
                link(dve.tensor_tensor(t[6], t[6], t[7], add))
                link(dve.reciprocal(t[6], t[6]))
                link(dve.tensor_tensor(t[6], t[6], co, mul))
                dve.tensor_tensor(t[8], t[0], t[4], mul)
                dve.tensor_tensor(t[9], t[2], t[5], mul)
                dve.tensor_tensor(t[10], t[2], t[4], mul)
                link(dve.tensor_tensor(t[11], t[0], t[5], mul))
                dve.tensor_tensor(t[8], t[8], t[9], add)
                link(dve.tensor_tensor(t[10], t[10], t[11], sub))
                dve.tensor_tensor(t[8], t[8], t[6], mul)
                link(dve.tensor_tensor(t[10], t[10], t[6], mul))
                dve.tensor_tensor(t[8], r00, t[8], sub)
                link(dve.tensor_tensor(t[10], i00, t[10], sub))
                dve.tensor_tensor(t[0], co, t[8], mul)
                dve.tensor_tensor(t[1], si, t[10], mul)
                dve.tensor_tensor(t[2], co, t[10], mul)
                link(dve.tensor_tensor(t[3], si, t[8], mul))
                dve.tensor_tensor(e[:, 1, :], t[0], t[1], sub)
                link(dve.tensor_tensor(e[:, 2, :], t[2], t[3], add))
                dve.tensor_scalar(e[:, 0, :], e[:, 2, :], -1.0, None, mul).then_inc(roots_done, 1)

            def kernel_columns():
                dve.wait_ge(dft_done, 1)
                y = e[:, 3:5, :].rearrange("p r m -> p (r m)")
                dve.tensor_copy(y, pg[0][:, 0:2 * M8]).then_inc(s4_read, 1)
                dve.wait_ge(s4_read, 2)
                prod = e[:, 5:21, :].rearrange("p a m -> p (a m)").rearrange("p (b i) -> p b i", b=M8)
                link(dve.tensor_tensor(prod, twiddle.rearrange("p (b i) -> p b i", b=M8),
                                       y[:, None, :].broadcast_to((P, M8, 2 * M8)), ALU.mult))
                link(dve.tensor_reduce(kcol[:, :], prod, AX.X, ALU.add))
                dve.tensor_tensor(kcol[0:1, 0:1], kcol[0:1, 0:1], d_sb[:, :], ALU.add).then_inc(kcol_done, 1)

            def group(g, first=False, tail=False, next_tail=False):
                for b in range(NB):
                    if first and b < 2:
                        for j in X_LATER[b]:
                            x_stats(j)
                            if j >= X_LATER[b][0] + 2:
                                x_low(j - 2)
                        for j in X_LATER[b][-2:]:
                            x_low(j)
                    if tail and b == 2:
                        roots()
                    h_mult(g, b, 0, first, tail)
                    if not tail:
                        if b == 1:
                            w_prep(g + 1, 1, next_tail)
                        if b == 3:
                            w_prep(g + 1, 4, next_tail)
                    h_mult(g, b, 1, first, tail)
                    if tail and b == 1:
                        cauchy_sums()
                    if tail and b == 2:
                        kernel_columns()
                    if tail and b == 3:
                        dve.wait_ge(kt_done, 1)
                        dve.tensor_copy(krow, pg[0][0:M8, 0:P]).then_inc(krow_done, 1)
                    if b == 0 and not first:
                        accumulate(g - 1, NB - 1)
                    if b >= 1:
                        accumulate(g, b - 1)
                    if tail and b == 0:
                        resolvent()
                    if not tail:
                        w_prep(g + 1, (0, 2, 3, 5)[b], next_tail)
            w_prep(0, 0, free=False)
            w_prep(0, 1, free=False)
            for j in range(4):
                x_stats(j)
            for j in range(2):
                x_low(j)
            w_prep(0, 2)
            for j in range(2, 4):
                x_low(j)
            w_prep(0, 3)
            w_prep(0, 4)
            w_prep(0, 5)
            group(0, first=True)
            with dve.Fori(0, (LOOP[1] - LOOP[0]) // 2) as it:
                for half_turn in range(2):
                    group(2 * it + (LOOP[0] + half_turn))
            group(NG - 1, next_tail=True)
            group(NG, tail=True)
            for n in range(2):
                for c in range(2):
                    dve.wait_ge(shi_done, 2 * n + c + 1)
                    dve.scalar_tensor_tensor(out=strip[:, 1, n, c * SB:(c + 1) * SB], in0=(pg, pu)[n][c][:, :],
                                             scalar=KS, in1=strip[:, 0, n, c * SB:(c + 1) * SB],
                                             op0=ALU.mult, op1=ALU.subtract).then_inc(slo_done, 1)
            accumulate(NG, NB - 1)
            for d in range(2 * NT):
                part = acc[:, d // 2, (d % 2) * SB:(d % 2 + 1) * SB]
                dve.wait_ge(conv_done, d + 1)
                dve.scalar_tensor_tensor(out=part, in0=po[d % 4][:, :], scalar=1.0 / (XS * KS), in1=part,
                                         op0=ALU.mult, op1=ALU.add).then_inc(conv_added, 1)


def _constants():
    l = np.arange(L)
    ang = np.pi * l / L
    angle = np.stack([np.cos(ang), np.sin(ang)])
    small = np.stack([np.cos(ang).reshape(P, M8), np.sin(ang).reshape(P, M8)], axis=1)
    a = np.arange(P)
    th = 2 * np.pi * np.outer(a, a) / P
    dft = np.stack([np.cos(th), np.sin(th)], axis=1)
    t = a[:, None, None] + P * np.arange(M8)[None, :, None]
    tw = 2 * np.pi * t * np.arange(M8)[None, None, :] / L
    twiddle = np.concatenate([np.cos(tw), -np.sin(tw)], axis=2) / L
    f = np.float32
    return {"ident": np.eye(P, dtype=f), "flip": np.eye(P, dtype=f)[::-1].copy(), "angle": angle.astype(f),
            "small": small.astype(f), "dft": dft.astype(f), "twiddle": twiddle.reshape(P, -1).astype(f)}


def _proj_words(wq):
    t = wq.T.reshape(4, P, I)
    main = t[:, :, :NG * CH].reshape(4, P, NG, P, 2).transpose(2, 1, 0, 4, 3).reshape(NG, P, 4 * CH)
    tail = t[:, :, NG * CH:].reshape(4, P, TAIL, 2).transpose(1, 0, 3, 2).reshape(P, 8 * TAIL)
    return main, tail


def _proj_sz(scale, zero):
    t = np.stack([scale.T, zero.T]).reshape(2, 4, 4, I)
    main = t[..., :NG * CH].reshape(2, 4, 4, NG, P, 2).transpose(3, 2, 1, 0, 5, 4).reshape(NG, 4, 8 * CH)
    tail = t[..., NG * CH:].reshape(2, 4, 4, TAIL, 2).transpose(2, 1, 0, 4, 3).reshape(4, 16 * TAIL)
    return main, tail


def _down_words(wq):
    t = wq.T
    return t[:NG * P].reshape(NG, P, H), t[NG * P:]


def _down_sz(scale, zero):
    t = np.stack([scale.T, zero.T]).reshape(2, I // GROUP, 2, H // 2)
    t = t.transpose(1, 2, 0, 3).reshape(I // GROUP, 2 * H)
    return t[:4 * NG].reshape(NG, 4, 2 * H), t[4 * NG:]


def kernel(**inputs):
    import concourse.bacc as _bacc
    from concourse.bass_utils import run_bass_kernel_spmd as _run

    a = {k.replace("L0_attn_", "").replace("L0_ffn_", ""): np.asarray(v) for k, v in inputs.items()}
    rg, tg = _proj_words(a["gate_Wq"])
    ru, tu = _proj_words(a["up_Wq"])
    rd, td = _down_words(a["down_Wq"])
    zg, tzg = _proj_sz(a["gate_scale"], a["gate_zero"])
    zu, tzu = _proj_sz(a["up_scale"], a["up_zero"])
    zd, tzd = _down_sz(a["down_scale"], a["down_zero"])
    arrays = {"x": a["u"].reshape(S, H), "raw_gate": rg, "raw_up": ru, "raw_down": rd,
              "sz_gate": zg, "sz_up": zu, "sz_down": zd,
              "tail_gate": tg, "tail_up": tu, "tail_down": td,
              "tsz_gate": tzg, "tsz_up": tzu, "tsz_down": tzd,
              "lam": a["Lambda_ri"], "p": a["p_ri"], "q": a["q_ri"], "vc": a["Vc_ri"],
              "ct": a["Ct_ri"].reshape(NS, 2), "bp": a["Bp"], "d": a["D"], "ls": a["log_step"]}
    arrays.update(_constants())
    nc = _bacc.Bacc("TRN2", target_bir_lowering=False, num_devices=1)
    feeds, args = {}, []
    for name, arr in arrays.items():
        arr = np.ascontiguousarray(arr)
        feeds[f"in_{name}"] = arr
        args.append(nc.dram_tensor(f"in_{name}", arr.shape, mybir.dt.from_np(arr.dtype), kind="ExternalInput").ap())
    out = nc.dram_tensor("out", (S, H), mybir.dt.float32, kind="ExternalOutput").ap()
    s4_plus_int4_swiglu(nc, *args, out)
    r = _run(nc, [feeds], core_ids=[0])
    return r.results[0]["out"].reshape(1, S, H)
```

```python
import numpy as np
import concourse.bass as bass
from concourse import mybir
from contextlib import ExitStack

S, H, I, NS = 2048, 1024, 2752, 64
P = 128
GROUP = 64
CH = 2 * P
NG = I // CH
TAIL = (I - NG * CH) // 2
TA = P - TAIL
TB = TAIL - TA
SB = 512
NB = S // SB
KC = H // P
NT = S // P
SLAB = 512
L = H
M8 = L // P

XS_LOG = 10
XS, WS = 2.0 ** XS_LOG, 2.0 ** 12
EPS = 1e-5


def s4_plus_int4_swiglu(nc, x_d, raw_gate, raw_up, raw_down, sz_gate, sz_up, sz_down,
                        tail_gate, tail_up, tail_down, tsz_gate, tsz_up, tsz_down,
                        lam_d, p_d, q_d, vc_d, ct_d, bp_d, d_d, ls_d,
                        ident_d, flip_d, angle_d, small_d, dft_d, twiddle_d, out_d):
    f32, f16, i32 = mybir.dt.float32, mybir.dt.float16, mybir.dt.int32
    ALU, ACT, AX = mybir.AluOpType, mybir.ActivationFunctionType, mybir.AxisListType

    ctx = ExitStack()
    with ctx:
        def sb(name, shape, dt=f32):
            return ctx.enter_context(nc.sbuf_tensor(name, shape, dt))

        def sem(name):
            return ctx.enter_context(nc.semaphore(name))

        acc = sb("acc", [P, NT, H])
        xh = sb("xh", [P, KC, S], f16)
        xl = sb("xl", [P, KC, S], f16)
        w_gu = [sb(f"w_gu{i}", [P, 2, 2, KC, CH], f16) for i in range(2)]
        w_dn = sb("w_dn", [P, 2, 2, H], f16)
        hh = sb("hh", [P, 2, 2, SB], f16)
        hl = sb("hl", [P, 2, 2, SB], f16)
        sil = sb("sil", [P, 2, SB])
        hf = sb("hf", [P, 2, SB])
        raw = sb("raw", [P, 2, SLAB], i32)
        sz = sb("sz", [P, 2, 2 * SLAB])
        wf = sb("wf", [P, 2, 2 * SLAB])
        ident = sb("ident", [P, P])
        stats = sb("stats", [P, 2, 2, 6])
        mv = sb("mv", [P, NT, 2])
        negm = sb("negm", [P, NT])
        vs = sb("vs", [P, NT])
        rstd = sb("rstd", [P, NT])
        nmr = sb("nmr", [P, NT])
        half = sb("half", [P, 1])
        par = sb("par", [P, 5, 2])
        vcb = sb("vcb", [P, NS, 2])
        bpb = sb("bpb", [P, NS])
        vw = sb("vw", [P, 8])
        sc = sb("sc", [P, 8])
        d_sb = sb("d_sb", [1, 1])
        cs8 = sb("cs8", [P, 2, M8])
        e = sb("e", [P, 24, M8])
        kcol = sb("kcol", [P, M8])
        zrow = sb("zrow", [1, 2 * P])
        kabs = sb("kabs", [P, M8])
        kmx = sb("kmx", [P, 1])
        ksc = sb("ksc", [P, 2], i32)
        xn = w_gu[1][:, :, :, :, :].rearrange("p a b k c -> p (a b k c)").bitcast(f32)\
            .rearrange("p (j h) -> p j h", j=4)
        s4w = w_gu[1][:, :, :, :, :].rearrange("p a b k c -> p (a b k c)").bitcast(f32)\
            .rearrange("p (j h) -> p j h", j=4)
        strip = w_gu[1][:, 0, :, :, :].rearrange("p b k c -> p b (k c)")\
            .rearrange("p b (n t) -> p b n t", n=2)
        angle = sz
        kshift = wf
        dft = raw[:, 0, 0:2 * P].bitcast(f32).rearrange("p (j a) -> p j a", j=2)
        flip = raw[:, 0, 2 * P:3 * P].bitcast(f32)
        twiddle = raw[:, 1, 0:P].bitcast(f32)
        krow = raw[0:M8, 1, P:2 * P].bitcast(f32)

        pg = [ctx.enter_context(nc.psum_tensor(f"pg{i}", [P, SB], f32)) for i in range(2)]
        pu = [ctx.enter_context(nc.psum_tensor(f"pu{i}", [P, SB], f32)) for i in range(2)]
        po = [ctx.enter_context(nc.psum_tensor(f"po{i}", [P, SB], f32)) for i in range(4)]

        kpad = nc.dram_tensor("kpad", [CH + L], f32, kind="Internal").ap()

        x_in = [sem(f"x_in{j}") for j in range(4 + NB - 1)]
        slab_in = [sem(f"slab_in{j}") for j in range(2)]
        ident_in, par_in, tab_in, kpad_out, kshift_in, out_done = \
            (sem(n) for n in ("ident_in", "par_in", "tab_in", "kpad_out", "kshift_in", "out_done"))
        consts, stat_done, rstd_done, xn_done, xt_done, xhi_done, xlo_done = \
            (sem(n) for n in ("consts", "stat_done", "rstd_done", "xn_done", "xt_done", "xhi_done", "xlo_done"))
        gate_done, up_done, down_done, silu_done, hf_done, hhi_done, hlo_done, acc_done = \
            (sem(n) for n in ("gate_done", "up_done", "down_done", "silu_done", "hf_done", "hhi_done",
                              "hlo_done", "acc_done"))
        wprep_done, whi_done, wlo_done, dve_order = \
            (sem(n) for n in ("wprep_done", "whi_done", "wlo_done", "dve_order"))
        dve_order_loop = sem("dve_order_loop")
        step_done, cauchy_done, s4_read, dft_done, krow_done, kzero_done, kt_done = \
            (sem(n) for n in ("step_done", "cauchy_done", "s4_read", "dft_done", "krow_done",
                              "kzero_done", "kt_done"))
        resolvent_done, roots_done, kcol_done, flip_done, shi_done, slo_done = \
            (sem(n) for n in ("resolvent_done", "roots_done", "kcol_done", "flip_done", "shi_done", "slo_done"))
        kabs_done, kscale_done = sem("kabs_done"), sem("kscale_done")
        conv_done, conv_added, pool_order = (sem(n) for n in ("conv_done", "conv_added", "pool_order"))

        def words(k, tail):
            return SLAB // 2 if tail and k in (2, 3) else SLAB

        def sz_view(slot, k, tail):
            w = words(k, tail)
            if k >= 4:
                v = sz[:, slot, 0:2 * w].rearrange("p (z w) -> p z w", z=2)
                return [v[:, z:z + 1, :].broadcast_to((P, 2, w)) for z in range(2)]
            v = sz[:, slot, 0:2 * w].rearrange("p (c z w) -> p c z w", c=2, z=2)
            return [v[:, None, :, z, :].broadcast_to((P, 2, 2, w // 2)) for z in range(2)]

        def wf_view(slot, k, tail, dt=f32):
            w = words(k, tail)
            v = wf[:, slot, 0:2 * w]
            v = v.bitcast(dt) if dt != f32 else v
            if k >= 4:
                return v.rearrange("p (a w) -> p a w", a=2)
            return v.rearrange("p (a c w) -> p a c w", a=2, c=2)

        def w_flat(slot, k, tail):
            w = words(k, tail)
            if k >= 4:
                return wf[:, slot, 0:2 * w].rearrange("p (a w) -> p a w", a=2)
            return wf[:, slot, 0:2 * w].rearrange("p (c w) -> p c w", c=4)

        def w_dest(parity, k, part, tail):
            if k >= 4 and tail:
                return w_dn[:, part, k - 4, :].rearrange("p (a w) -> p a w", a=2)
            if k >= 4:
                return w_dn[:, part, :, (k - 4) * SLAB:(k - 3) * SLAB]
            return w_gu[parity][:, k // 2, part, 4 * (k % 2):4 * (k % 2) + 4, 0:words(k, tail) // 2]

        FIRST = 0
        LOOP = (1, NG - 1)

        block = ctx.enter_context(nc.Block())

        @block.sync
        def _(sp):
            def load_slab(g, k, tail=False, free=True):
                slot = k % 2
                if free:
                    sp.wait_ge(wprep_done, 6 * g + k - 1)
                w = words(k, tail)
                if tail:
                    r = (tail_gate, tail_up)[k // 2][:, (k % 2) * w:(k % 2 + 1) * w]
                    z = (tsz_gate, tsz_up)[k // 2][:, (k % 2) * 2 * w:(k % 2 + 1) * 2 * w]
                else:
                    r = (raw_gate, raw_up, raw_down)[k // 2]
                    z = (sz_gate, sz_up, sz_down)[k // 2]
                    r = r[bass.ds(g, 1), :, (k % 2) * w:(k % 2 + 1) * w].rearrange("g p w -> (g p) w")
                    z = z[bass.ds(g, 1), :, (k % 2) * 2 * w:(k % 2 + 1) * 2 * w].rearrange("g q w -> (g q) w")
                sp.dma_start(raw[:, slot, 0:w], r).then_inc(slab_in[slot], 16)
                sp.dma_start(sz[:, slot, 0:2 * w], z[:, None, :].broadcast_to((4, 32, 2 * w)))\
                    .then_inc(slab_in[slot], 16)

            def load_tail_down(k):
                sp.wait_ge(wprep_done, 6 * NG + k)
                parts = ((0, TAIL, 0), (TAIL, P, 0)) if k == 4 else ((0, TB, TA), (TB, P, TA))
                for p0, p1, row in parts:
                    n = p1 - p0
                    sp.dma_start(raw[p0:p1, :, :].rearrange("p a w -> p (a w)"), tail_down[row:row + n, :])\
                        .then_inc(slab_in[k % 2], 16)
                    z = tsz_down[row // 32:(row + n) // 32, :]
                    sp.dma_start(sz[p0:p1, :, :].rearrange("p a w -> p (a w)"),
                                 z[:, None, :].broadcast_to((n // 32, 32, 2 * H))).then_inc(slab_in[k % 2], 16)

            def load_x(b):
                sp.dma_start(acc[:, 4 * b:4 * b + 4, :],
                             x_d[b * SB:(b + 1) * SB, :].rearrange("(j p) h -> p j h", p=P)).then_inc(x_in[3 + b], 16)

            def load_x_tile(j):
                sp.dma_start(acc[:, j, :], x_d[j * P:(j + 1) * P, :]).then_inc(x_in[j], 16)

            load_x_tile(0)
            load_x_tile(1)
            load_slab(0, 0, free=False)
            load_x_tile(2)
            load_x_tile(3)
            load_slab(0, 1, free=False)
            load_slab(0, 2)
            load_x(1)
            load_slab(0, 3)
            load_x(2)
            load_slab(0, 4)
            load_x(3)
            load_slab(0, 5)
            for h2 in range(2):
                for i, src in enumerate((lam_d, p_d, q_d, ct_d)):
                    sp.dma_start(par[h2 * NS:(h2 + 1) * NS, i, :], src).then_inc(par_in, 16)
                sp.dma_start(vcb[h2 * NS:(h2 + 1) * NS, :, :], vc_d).then_inc(par_in, 16)
            sp.dma_start(bpb[:, :], bp_d.rearrange("n a -> a n").broadcast_to((P, NS))).then_inc(par_in, 16)
            sp.dma_start(sc[:, 0:1], ls_d[:, None].broadcast_to((P, 1))).then_inc(par_in, 16)
            sp.dma_start(d_sb[:, :], d_d[:, None]).then_inc(par_in, 16)
            for k in range(6):
                load_slab(1, k)
            with sp.Fori(0, (LOOP[1] - LOOP[0]) // 2) as it:
                for half_turn in range(2):
                    for k in range(6):
                        load_slab(2 * it + (LOOP[0] + half_turn + 1), k)
            for k in range(4):
                load_slab(NG, k, tail=True)
            load_tail_down(4)
            load_tail_down(5)
            sp.wait_ge(wprep_done, 6 * NG + 6)
            for j in range(2):
                sp.dma_start(angle[:, j, :], angle_d[j:j + 1, :].broadcast_to((P, L))).then_inc(tab_in, 16)
            sp.dma_start(dft, dft_d).then_inc(tab_in, 16)
            sp.dma_start(flip, flip_d).then_inc(tab_in, 16)
            sp.dma_start(twiddle, twiddle_d).then_inc(tab_in, 16)
            sp.dma_start(cs8[:, :, :], small_d).then_inc(tab_in, 16)
            sp.wait_ge(kzero_done, 1)
            sp.dma_start(kpad[0:CH][None, :], zrow[0:1, :]).then_inc(kpad_out, 16)
            sp.wait_ge(krow_done, 1)
            sp.dma_start(kpad[CH:CH + L].rearrange("(b a) -> b a", b=M8), krow).then_inc(kpad_out, 16)
            sp.wait_ge(kpad_out, 32)
            for n in range(2):
                src = bass.AP(kpad.tensor, 2 - n, [[2, P], [1, L]])
                sp.dma_start(kshift[:, n, :], src).then_inc(kshift_in, 16)
            for st in range(NT - 1):
                sp.wait_ge(conv_added, 2 * st + 2)
                sp.dma_start(out_d[st * P:(st + 1) * P, :], acc[:, st, :]).then_inc(out_done, 16)
            for c in range(2):
                sp.wait_ge(conv_added, 2 * NT - 1 + c)
                sp.dma_start(out_d[S - P:S, c * SB:(c + 1) * SB], acc[:, NT - 1, c * SB:(c + 1) * SB])\
                    .then_inc(out_done, 16)
            sp.wait_ge(out_done, 16 * (NT + 1))

        @block.gpsimd
        def _(pool):
            pool.memset(half[:, :], -0.5).then_inc(pool_order, 1)
            pool.memset(zrow[:, :], 0.0).then_inc(kzero_done, 1)
            pool.memset(sc[:, 7:8], float(np.e)).then_inc(pool_order, 1)
            pool.wait_ge(pool_order, 2)

            def x_rstd(j):
                pool.wait_ge(stat_done, j + 1)
                pool.tensor_tensor(rstd[:, j:j + 1], vs[:, j:j + 1], half[:, :], ALU.pow).then_inc(pool_order, 1)
                pool.wait_ge(pool_order, j + 3)
                pool.tensor_tensor(nmr[:, j:j + 1], negm[:, j:j + 1], rstd[:, j:j + 1], ALU.mult)\
                    .then_inc(rstd_done, 1)

            def w_low(g, k, parity, tail=False):
                pool.wait_ge(whi_done, 6 * g + k + 1)
                pool.tensor_tensor(w_dest(parity, k, 1, tail), w_flat(k % 2, k, tail), w_dest(parity, k, 0, tail),
                                   ALU.subtract).then_inc(wlo_done, 1)

            def h_low(g, b, t, tail=False):
                r0 = TB if tail and t == 1 else 0
                if tail:
                    pool.wait_ge(hlo_done, 8 * g + 2 * b + t)
                pool.wait_ge(hhi_done, 8 * g + 2 * b + t + 1)
                pool.tensor_tensor(hl[r0:P, b % 2, t, :], hf[r0:P, t, :], hh[r0:P, b % 2, t, :],
                                   ALU.subtract).then_inc(hlo_done, 1)

            def first_group():
                for j in range(3):
                    x_rstd(j)
                w_low(0, 0, 0)
                x_rstd(3)
                for k in range(1, 4):
                    w_low(0, k, 0)
                for j in range(4, 8):
                    x_rstd(j)
                h_low(0, 0, 0)
                x_rstd(8)
                h_low(0, 0, 1)
                x_rstd(9)
                w_low(0, 4, 0)
                x_rstd(10)
                x_rstd(11)
                h_low(0, 1, 0)
                x_rstd(12)
                h_low(0, 1, 1)
                x_rstd(13)
                w_low(0, 5, 0)
                x_rstd(14)
                x_rstd(15)
                h_low(0, 2, 0)
                h_low(0, 2, 1)
                w_low(1, 0, 1)
                w_low(1, 1, 1)
                h_low(0, 3, 0)
                w_low(1, 2, 1)
                h_low(0, 3, 1)
                w_low(1, 3, 1)

            def group(g, parity, tail=False, next_tail=False):
                for b in range(NB):
                    h_low(g, b, 0, tail)
                    if not tail:
                        if b == 1:
                            w_low(g + 1, 0, 1 - parity, next_tail)
                        if b == 3:
                            w_low(g + 1, 3, 1 - parity, next_tail)
                    h_low(g, b, 1, tail)
                    if not tail and b == 2:
                        w_low(g + 1, 1, 1 - parity, next_tail)
                        w_low(g + 1, 2, 1 - parity, next_tail)
                    if tail:
                        pool.wait_ge(hlo_done, 8 * g + 2 * b + 2)
                    if b == 0:
                        w_low(g, 4, parity, tail)
                        w_low(g, 5, parity, tail)
                    if tail and b == 2:
                        pool.wait_ge(kcol_done, 1)
                        pool.partition_all_reduce(kabs[:, :], kcol[:, :], P, bass.bass_isa.ReduceOp.absmax)\
                            .then_inc(kabs_done, 1)

            first_group()
            pool.wait_ge(par_in, 16 * 13)
            pool.tensor_tensor(sc[:, 1:2], sc[:, 7:8], sc[:, 0:1], ALU.pow).then_inc(step_done, 1)
            with pool.Fori(0, (LOOP[1] - LOOP[0]) // 2) as it:
                for half_turn in range(2):
                    group(2 * it + (LOOP[0] + half_turn), (LOOP[0] + half_turn) % 2)
            group(NG - 1, (NG - 1) % 2, next_tail=True)
            group(NG, NG % 2, tail=True)

        @block.scalar
        def _(act):
            act.dma_start(ident[:, :], ident_d).then_inc(ident_in, 16)

            def normalize(j):
                act.wait_ge(rstd_done, j + 1)
                act.wait_ge(x_in[min(j, 3 + j // 4)], 16)
                if j >= 4:
                    act.wait_ge(xt_done, 2 * j - 6)
                act.activation(xn[:, j % 4, :], acc[:, j, :], ACT.Identity, scale=rstd[:, j:j + 1],
                               bias=nmr[:, j:j + 1]).then_inc(xn_done, 1)

            def x_high(j):
                for hf2 in range(2):
                    act.wait_ge(xt_done, 2 * j + hf2 + 1)
                    act.activation(xh[:, 4 * hf2:4 * hf2 + 4, j * P:(j + 1) * P],
                                   po[2 * (j % 2) + hf2][:, :].rearrange("p (k s) -> p k s", k=4),
                                   ACT.Copy).then_inc(xhi_done, 1)

            def w_high(g, k, parity, tail=False):
                act.wait_ge(wprep_done, 6 * g + k + 1)
                if g is not FIRST:
                    if k < 4:
                        act.wait_ge(up_done, 8 * g - 8)
                    else:
                        act.wait_ge(down_done, 32 * g)
                act.activation(w_dest(parity, k, 0, tail), w_flat(k % 2, k, tail), ACT.Copy)\
                    .then_inc(whi_done, 1)

            def silu(g, b, t, tail):
                idx = 8 * g + 2 * b + t
                act.wait_ge(gate_done, idx + 1)
                if not (g is FIRST and b == 0):
                    act.wait_ge(hf_done, idx - 1)
                if tail and t == 1:
                    out, gate = sil[TB:P, t, :], pg[t][0:TB, :]
                else:
                    out, gate = sil[:, t, :], pg[t][:, :]
                act.activation(out, gate, ACT.Silu, scale=1.0 / (XS * WS)).then_inc(silu_done, 1)

            def h_high(g, b, t, tail):
                act.wait_ge(hf_done, 8 * g + 2 * b + t + 1)
                if not (g is FIRST and b < 2):
                    act.wait_ge(down_done, 32 * g + 8 * b - 8)
                if tail and t == 1:
                    act.activation(hl[0:TB, b % 2, t, :], hf[TB:P, t, :], ACT.Copy)
                    act.activation(hh[TB:P, b % 2, t, :], hf[TB:P, t, :], ACT.Copy).then_inc(hhi_done, 1)
                else:
                    act.activation(hh[:, b % 2, t, :], hf[:, t, :], ACT.Copy).then_inc(hhi_done, 1)

            def first_group():
                for j in (0, 1):
                    normalize(j)
                x_high(0)
                w_high(0, 0, 0)
                normalize(2)
                x_high(1)
                normalize(3)
                x_high(2)
                x_high(3)
                for k in range(1, 4):
                    w_high(0, k, 0)
                normalize(4)
                normalize(5)
                for b in range(3):
                    for t in range(2):
                        j = 4 * b + 4 + 2 * t
                        if t == 0:
                            normalize(j + 2)
                        elif b < 2:
                            normalize(j + 1)
                            normalize(j + 2)
                        else:
                            normalize(j + 1)
                        x_high(j)
                        x_high(j + 1)
                        silu(0, b, t, False)
                        if b < 2:
                            h_high(0, b, t, False)
                        if t == 1 and b < 2:
                            normalize(j + 3)
                            w_high(0, 4 + b, 0)
                h_high(0, 2, 0, False)
                h_high(0, 2, 1, False)
                act.wait_ge(xt_done, 2 * NT)
                w_high(1, 0, 1)
                w_high(1, 1, 1)
                silu(0, 3, 0, False)
                h_high(0, 3, 0, False)
                w_high(1, 2, 1)
                silu(0, 3, 1, False)
                h_high(0, 3, 1, False)
                w_high(1, 3, 1)

            def group(g, parity, tail=False, next_tail=False):
                for b in range(NB):
                    silu(g, b, 0, tail)
                    h_high(g, b, 0, tail)
                    if not tail:
                        if b == 1:
                            w_high(g + 1, 0, 1 - parity, next_tail)
                        if b == 3:
                            w_high(g + 1, 3, 1 - parity, next_tail)
                    silu(g, b, 1, tail)
                    h_high(g, b, 1, tail)
                    if not tail and b == 2:
                        w_high(g + 1, 1, 1 - parity, next_tail)
                        w_high(g + 1, 2, 1 - parity, next_tail)
                    if b == 0:
                        w_high(g, 4, parity, tail)
                        w_high(g, 5, parity, tail)

            first_group()
            with act.Fori(0, (LOOP[1] - LOOP[0]) // 2) as it:
                for half_turn in range(2):
                    group(2 * it + (LOOP[0] + half_turn), (LOOP[0] + half_turn) % 2)
            group(NG - 1, (NG - 1) % 2, next_tail=True)
            group(NG, NG % 2, tail=True)
            act.wait_ge(kscale_done, 1)
            for n in range(2):
                for c in range(2):
                    act.wait_ge(flip_done, 2 * n + c + 1)
                    act.activation(strip[:, 0, n, c * SB:(c + 1) * SB], (pg, pu)[n][c][:, :], ACT.Copy,
                                   scale=ksc[:, 0:1].bitcast(f32)).then_inc(shi_done, 1)

        @block.tensor
        def _(pe):
            pe.wait_ge(ident_in, 16)

            def x_transpose(j):
                pe.wait_ge(xn_done, j + 1)
                for hf2 in range(2):
                    if j >= 2:
                        pe.wait_ge(xlo_done, 2 * j + hf2 - 3)
                    for kk in range(4):
                        first_h = 2 * P * (2 * hf2 + kk % 2) + kk // 2
                        last = pe.transpose(po[2 * (j % 2) + hf2][:, kk * P:(kk + 1) * P],
                                            xn[:, j % 4, first_h:first_h + 2 * P - 1:2], ident[:, :])
                    last.then_inc(xt_done, 1)

            def project(g, b, t, mat, parity, first):
                idx = 8 * g + 2 * b + t
                bank = (pg, pu)[mat][t]
                if not (first and b == 0):
                    pe.wait_ge((silu_done, hf_done)[mat], idx - 1)
                w = w_gu[parity]
                toks = slice(b * SB, (b + 1) * SB)
                for k in range(KC):
                    if first and b == 0 and t == 0 and k % 4 == 0:
                        pe.wait_ge(wlo_done, 2 * mat + k // 4 + 1)
                    for wp, xp in ((0, xh), (0, xl), (1, xh)):
                        last = pe.matmul(bank[:, :], w[:, mat, wp, k, t * P:(t + 1) * P], xp[:, k, toks],
                                         start=(k == 0 and wp == 0 and xp is xh), stop=(k == KC - 1 and wp == 1))
                last.then_inc((gate_done, up_done)[mat], 1)

            def down(g, b, tail=False, first=False):
                pe.wait_ge(hlo_done, 8 * g + 2 * b + 2)
                for d in range(8):
                    st, hd = d // 2, d % 2
                    if not (first and b == 0 and d < 4):
                        pe.wait_ge(acc_done, 32 * g + 8 * b + d - 3)
                    steps = [(t, hp, P, wp) for t in range(2) for hp, wp in ((hh, 0), (hh, 1), (hl, 0))]
                    if tail:
                        steps[3:] = [(1, hl, P, 0), (1, hl, TB, 1)]
                    for i, (t, hp, n, wp) in enumerate(steps):
                        last = pe.matmul(po[d % 4][:, :], hp[0:n, b % 2, t, st * P:(st + 1) * P],
                                         w_dn[0:n, wp, t, hd * SB:(hd + 1) * SB],
                                         start=(i == 0), stop=(i == len(steps) - 1))
                    last.then_inc(down_done, 1)

            def tail_project(b, piece, parity):
                t = piece // 2
                if piece == 1:
                    bank, mat = pu[b % 2], 1
                    pe.wait_ge(hf_done, 8 * NG + max(2 * b - 2, b - 1))
                else:
                    bank, mat = pg[t], 0
                    pe.wait_ge(hf_done, 8 * NG + 2 * b + t - 1)
                for k in range(KC):
                    for wp, xp in ((0, xh), (0, xl), (1, xh)):
                        last = pe.matmul(bank[:, :], w_gu[parity][:, mat, wp, k, t * P:(t + 1) * P],
                                         xp[:, k, b * SB:(b + 1) * SB],
                                         start=(k == 0 and wp == 0 and xp is xh), stop=(k == KC - 1 and wp == 1))
                last.then_inc((gate_done, up_done)[mat], 1)

            def group(g, parity):
                for b in range(NB):
                    for t in range(2):
                        for mat in range(2):
                            if b == 0 and t == 0:
                                pe.wait_ge(wlo_done, 6 * g + 2 + 2 * mat)
                            project(g, b, t, mat, parity, False)
                    if b == 0:
                        down(g - 1, NB - 1)
                    else:
                        if b == 1:
                            pe.wait_ge(wlo_done, 6 * g + 6)
                        down(g, b - 1)

            def first_group():
                for j in range(4):
                    x_transpose(j)
                for b in range(NB):
                    pe.wait_ge(xlo_done, 8 * b + 8)
                    for mat in range(2):
                        project(0, b, 0, mat, 0, True)
                    if b < 3:
                        x_transpose(4 * b + 4)
                        x_transpose(4 * b + 5)
                    project(0, b, 1, 0, 0, True)
                    if b < 3:
                        x_transpose(4 * b + 6)
                        x_transpose(4 * b + 7)
                    project(0, b, 1, 1, 0, True)
                    if b == 2:
                        pe.wait_ge(xlo_done, 2 * NT)
                        pe.wait_ge(wlo_done, 6)
                        down(0, 0, first=True)
                        down(0, 1)
                down(0, 2)

            def tail_group(parity):
                for b in range(NB):
                    for piece in range(3):
                        if b == 0:
                            pe.wait_ge(wlo_done, 6 * NG + 2 + 2 * min(piece, 1))
                        if b >= 2 and piece == 4 - 2 * (b - 1):
                            pe.wait_ge(s4_read, b - 1)
                        tail_project(b, piece, parity)
                    if b >= 2:
                        s4_steps(b)
                    if b == 0:
                        down(NG - 1, NB - 1)
                    else:
                        if b == 1:
                            pe.wait_ge(wlo_done, 6 * NG + 6)
                        down(NG, b - 1, True)
                    if b == 1:
                        s4_steps(b)

            def s4_steps(b):
                if b == 1:
                    pe.wait_ge(resolvent_done, 1)
                    pe.wait_ge(hf_done, 8 * NG + 4)
                    for m in range(M8):
                        last = pe.matmul(pg[1][:, 8 * m:8 * m + 8], s4w[:, 2, m:L:M8], vw[:, :],
                                         start=True, stop=True)
                    last.then_inc(cauchy_done, 1)
                if b == 2:
                    pe.wait_ge(roots_done, 1)
                    pe.wait_ge(hf_done, 8 * NG + 5)
                    pe.matmul(pg[0][:, 0:2 * M8], dft[:, 0, :], e[:, 1:3, :], start=True, stop=False)
                    pe.matmul(pg[0][:, 0:2 * M8], dft[:, 1, :], e[:, 0:2, :], start=False, stop=True)\
                        .then_inc(dft_done, 1)
                if b == 3:
                    pe.wait_ge(kcol_done, 1)
                    pe.wait_ge(hf_done, 8 * NG + 7)
                    pe.transpose(pg[0][0:M8, 0:P], kcol[:, :], ident[:, :]).then_inc(kt_done, 1)

            first_group()
            with pe.Fori(0, (LOOP[1] - LOOP[0]) // 2) as it:
                for half_turn in range(2):
                    group(2 * it + (LOOP[0] + half_turn), (LOOP[0] + half_turn) % 2)
            group(NG - 1, (NG - 1) % 2)
            tail_group(NG % 2)
            pe.wait_ge(kshift_in, 32)
            pe.wait_ge(hf_done, 8 * NG + 8)
            pe.wait_ge(krow_done, 1)
            for n in range(2):
                for c in range(2):
                    pe.matmul((pg, pu)[n][c][:, :], flip, kshift[:, n, c * SB:(c + 1) * SB],
                              start=True, stop=True).then_inc(flip_done, 1)
            down(NG, NB - 1, True)
            pe.wait_ge(slo_done, 4)
            for st in range(NT):
                for c in range(2):
                    d = 2 * st + c
                    pe.wait_ge(acc_done, 32 * (NG + 1) - 3 + min(d, 3))
                    if d >= 4:
                        pe.wait_ge(conv_added, d - 3)
                    chunks = [k for k in range(KC) if 2 * P * (2 * (k // 4) + k % 2) < (c + 1) * SB]
                    for k in chunks:
                        h0, nib = 2 * P * (2 * (k // 4) + k % 2), (k // 2) % 2
                        t0 = max(c * SB, h0)
                        for xp, sp_ in ((xh, 0), (xh, 1), (xl, 0)):
                            last = pe.matmul(po[d % 4][:, t0 - c * SB:SB], xp[:, k, st * P:(st + 1) * P],
                                             strip[:, sp_, nib, t0 - h0:(c + 1) * SB - h0],
                                             start=(k == 0 and xp is xh and sp_ == 0),
                                             stop=(k == chunks[-1] and xp is xl))
                    last.then_inc(conv_done, 1)

        @block.vector
        def _(dve):
            chain = [0]

            def link(ins):
                chain[0] += 1
                ins.then_inc(dve_order, 1)
                dve.wait_ge(dve_order, chain[0])

            def x_stats(j):
                dve.wait_ge(x_in[min(j, 3 + j // 4)], 16)
                for c in range(2):
                    last = dve.bn_stats(stats[:, j % 2, c, :], acc[:, j, c * SB:(c + 1) * SB])
                link(last)
                link(dve.bn_aggr(mv[:, j, :], stats[:, j % 2, :, :].rearrange("p c s -> p (c s)")))
                link(dve.tensor_scalar(negm[:, j:j + 1], mv[:, j, 0:1], -1.0, None, ALU.mult))
                dve.tensor_scalar(vs[:, j:j + 1], mv[:, j, 1:2], XS ** -2, EPS * XS ** -2, ALU.mult, ALU.add)\
                    .then_inc(stat_done, 1)

            def x_low(j):
                for hf2 in range(2):
                    dst = (slice(None), slice(4 * hf2, 4 * hf2 + 4), slice(j * P, (j + 1) * P))
                    dve.wait_ge(xhi_done, 2 * j + hf2 + 1)
                    dve.tensor_tensor(xl[dst], po[2 * (j % 2) + hf2][:, :].rearrange("p (k s) -> p k s", k=4),
                                      xh[dst], ALU.subtract).then_inc(xlo_done, 1)

            def tail_down_prep(k):
                slot, n = k % 2, 6 * NG + k
                dve.wait_ge(slab_in[slot], 96 * NG + 64 + 64)
                dve.wait_ge(wlo_done, n - 1)
                r = raw[:, :, :].rearrange("p a w -> p (a w)")
                q, w = wf[:, slot, :].bitcast(i32), wf[:, slot, :]
                z = sz[:, :, :]
                if k == 4:
                    dve.tensor_scalar(q[0:TAIL], r[0:TAIL], 4, 15, ALU.arith_shift_right, ALU.bitwise_and)
                    last = dve.tensor_scalar(q[TAIL:P], r[TAIL:P], 15, None, ALU.bitwise_and)
                else:
                    last = dve.tensor_scalar(q, r, 15, None, ALU.bitwise_and)
                last.then_inc(dve_order_loop, 1)
                dve.wait_ge(dve_order_loop, 2 * n + 1)
                dve.tensor_tensor(w, q, z[:, 1, :], ALU.subtract).then_inc(dve_order_loop, 1)
                dve.wait_ge(dve_order_loop, 2 * n + 2)
                dve.scalar_tensor_tensor(out=w, in0=w, scalar=WS, in1=z[:, 0, :], op0=ALU.mult, op1=ALU.mult)\
                    .then_inc(wprep_done, 1)

            def w_prep(g, k, tail=False, free=True):
                slot, n = k % 2, 6 * g + k
                dve.wait_ge(slab_in[slot], 32 * 3 * g + 32 * (k // 2 + 1))
                if free:
                    dve.wait_ge(wlo_done, n - 1)
                q = wf_view(slot, k, tail, i32)
                w = wf_view(slot, k, tail)
                r = raw[:, slot, 0:words(k, tail)]
                if k < 4:
                    r = r.rearrange("p (c w) -> p c w", c=2)
                scale, zero = sz_view(slot, k, tail)
                dve.tensor_scalar(q[:, 0], r, 4, 15, ALU.arith_shift_right, ALU.bitwise_and)
                dve.tensor_scalar(q[:, 1], r, 15, None, ALU.bitwise_and).then_inc(dve_order_loop, 1)
                dve.wait_ge(dve_order_loop, 2 * n + 1)
                dve.tensor_tensor(w, q, zero, ALU.subtract).then_inc(dve_order_loop, 1)
                dve.wait_ge(dve_order_loop, 2 * n + 2)
                for nib in range(2):
                    last = dve.scalar_tensor_tensor(out=w[:, nib], in0=w[:, nib], scalar=WS, in1=scale[:, nib],
                                                    op0=ALU.mult, op1=ALU.mult)
                last.then_inc(wprep_done, 1)

            def tail_h_mult(b, t):
                if t == 0:
                    dve.wait_ge(up_done, 8 * NG + b + 1)
                dve.wait_ge(silu_done, 8 * NG + 2 * b + t + 1)
                dve.wait_ge(hlo_done, 8 * NG + 2 * b + t - 1)
                r0, up = ((0, pu[b % 2][:, :]), (TB, pg[1][TB:P, :]))[t]
                dve.scalar_tensor_tensor(out=hf[r0:P, t, :], in0=up, scalar=1.0 / (XS * WS),
                                         in1=sil[r0:P, t, :], op0=ALU.mult, op1=ALU.mult).then_inc(hf_done, 1)

            def h_mult(g, b, t):
                idx = 8 * g + 2 * b + t
                dve.wait_ge(up_done, idx + 1)
                dve.wait_ge(silu_done, idx + 1)
                if not (g is FIRST and b == 0):
                    dve.wait_ge(hlo_done, idx - 1)
                dve.scalar_tensor_tensor(out=hf[:, t, :], in0=pu[t][:, :], scalar=1.0 / (XS * WS),
                                         in1=sil[:, t, :], op0=ALU.mult, op1=ALU.mult).then_inc(hf_done, 1)

            def accumulate(g, b):
                for d in range(8):
                    part = acc[:, 4 * b + d // 2, (d % 2) * SB:(d % 2 + 1) * SB]
                    dve.wait_ge(down_done, 32 * g + 8 * b + d + 1)
                    dve.scalar_tensor_tensor(out=part, in0=po[d % 4][:, :], scalar=1.0 / WS, in1=part,
                                             op0=ALU.mult, op1=ALU.add).then_inc(acc_done, 1)

            def numerators():
                dve.wait_ge(par_in, 16 * 13)
                dve.wait_ge(step_done, 1)
                t3 = e[:, 0:16, :].rearrange("p a m -> p (a m)").rearrange("p (r n) -> p r n", r=2)
                link(dve.tensor_tensor(t3, vcb[:, :, :].rearrange("p n r -> p r n"),
                                       bpb[:, None, :].broadcast_to((P, 2, NS)), ALU.mult))
                link(dve.tensor_reduce(par[:, 4, :], t3, AX.X, ALU.add))
                ar = e[:, 16, 0:2]
                ai = e[:, 16, 2:4]
                br = e[:, 16, 4:6]
                bi = e[:, 16, 6:8]
                for dst, src in ((ar, (3, 2)), (br, (4, 1))):
                    for j in range(2):
                        dve.tensor_copy(dst[:, j:j + 1], par[:, src[j], 0:1])
                for dst, src in ((ai, (3, 2)), (bi, (4, 1))):
                    for j in range(2):
                        last = dve.tensor_copy(dst[:, j:j + 1], par[:, src[j], 1:2])
                link(last)

                def outer(a, b_):
                    return a[:, :, None].broadcast_to((P, 2, 2)), b_[:, None, :].broadcast_to((P, 2, 2))

                m = [e[:, 17 + j // 2, 4 * (j % 2):4 * (j % 2) + 4].rearrange("p (a b) -> p a b", a=2)
                     for j in range(4)]
                for o, (a, b_) in zip(m, ((ar, br), (ai, bi), (ar, bi), (ai, br))):
                    i0, i1 = outer(a, b_)
                    last = dve.tensor_tensor(o, i0, i1, ALU.mult)
                link(last)
                v = [e[:, 19, 4 * j:4 * j + 4].rearrange("p (a b) -> p a b", a=2) for j in range(2)]
                dve.tensor_tensor(v[0], m[0], m[1], ALU.add)
                link(dve.tensor_tensor(v[1], m[2], m[3], ALU.subtract))
                dve.tensor_copy(vw[0:NS, :], e[0:NS, 19, :])
                dve.tensor_scalar(vw[NS:P, 0:4], e[NS:P, 19, 4:8], -1.0, None, ALU.mult)
                dve.tensor_copy(vw[NS:P, 4:8], e[NS:P, 19, 0:4])
                link(dve.reciprocal(sc[:, 2:3], sc[:, 1:2]))
                link(dve.tensor_scalar(sc[:, 2:3], sc[:, 2:3], 2.0, None, ALU.mult))
                dve.tensor_scalar(sc[:, 3:5], par[:, 0, :], -1.0, None, ALU.mult)
                dve.tensor_scalar(sc[0:NS, 5:6], par[0:NS, 0, 0:1], -1.0, None, ALU.mult)
                dve.tensor_copy(sc[NS:P, 5:6], par[NS:P, 0, 1:2])
                dve.memset(sc[0:NS, 6:7], 0.0)
                link(dve.tensor_scalar(sc[NS:P, 6:7], sc[NS:P, 2:3], -1.0, None, ALU.mult))

            def denominators():
                dve.wait_ge(tab_in, 16 * 6)
                dve.wait_ge(up_done, 8 * NG)
                re, im, res = s4w[:, 0, :], s4w[:, 1, :], s4w[:, 2, :]
                dve.tensor_scalar(re, angle[:, 0, :], sc[:, 3:4], None, ALU.mult)
                dve.tensor_scalar(im, angle[:, 1, :], sc[:, 2:3], None, ALU.mult)
                link(dve.tensor_scalar(res, angle[:, 0, :], sc[:, 5:6], None, ALU.mult))
                dve.scalar_tensor_tensor(out=im, in0=angle[:, 0, :], scalar=sc[:, 4:5], in1=im,
                                         op0=ALU.mult, op1=ALU.add)
                link(dve.scalar_tensor_tensor(out=res, in0=angle[:, 1, :], scalar=sc[:, 6:7], in1=res,
                                              op0=ALU.mult, op1=ALU.add))
                dve.tensor_tensor(re, re, re, ALU.mult)
                link(dve.tensor_tensor(im, im, im, ALU.mult))
                link(dve.tensor_tensor(re, re, im, ALU.add))

            def resolvent():
                re, res = s4w[:, 0, :], s4w[:, 2, :]
                link(dve.reciprocal(re, re))
                dve.tensor_tensor(res, res, re, ALU.mult).then_inc(resolvent_done, 1)

            def cauchy_sums():
                dve.wait_ge(cauchy_done, 1)
                sums = pg[1][:, 0:8 * M8].rearrange("p (m j) -> p j m", j=8)
                dve.tensor_copy(e[:, 3:11, :], sums).then_inc(s4_read, 1)

            def roots():
                dve.wait_ge(s4_read, 1)
                r00, r01, r10, r11, i00, i01, i10, i11 = (e[:, 3 + j, :] for j in range(8))
                co, si = cs8[:, 0, :], cs8[:, 1, :]
                t = [e[:, 11 + j, :] for j in range(13)]
                mul, add, sub = ALU.mult, ALU.add, ALU.subtract
                dve.tensor_tensor(t[0], r01, r10, mul)
                dve.tensor_tensor(t[1], i01, i10, mul)
                dve.tensor_tensor(t[2], r01, i10, mul)
                dve.tensor_tensor(t[3], i01, r10, mul)
                dve.tensor_tensor(t[4], co, r11, mul)
                link(dve.tensor_tensor(t[5], co, i11, mul))
                dve.tensor_tensor(t[0], t[0], t[1], sub)
                dve.tensor_tensor(t[2], t[2], t[3], add)
                link(dve.tensor_scalar(t[4], t[4], 1.0, None, add))
                dve.tensor_tensor(t[6], t[4], t[4], mul)
                link(dve.tensor_tensor(t[7], t[5], t[5], mul))
                link(dve.tensor_tensor(t[6], t[6], t[7], add))
                link(dve.reciprocal(t[6], t[6]))
                link(dve.tensor_tensor(t[6], t[6], co, mul))
                dve.tensor_tensor(t[8], t[0], t[4], mul)
                dve.tensor_tensor(t[9], t[2], t[5], mul)
                dve.tensor_tensor(t[10], t[2], t[4], mul)
                link(dve.tensor_tensor(t[11], t[0], t[5], mul))
                dve.tensor_tensor(t[8], t[8], t[9], add)
                link(dve.tensor_tensor(t[10], t[10], t[11], sub))
                dve.tensor_tensor(t[8], t[8], t[6], mul)
                link(dve.tensor_tensor(t[10], t[10], t[6], mul))
                dve.tensor_tensor(t[8], r00, t[8], sub)
                link(dve.tensor_tensor(t[10], i00, t[10], sub))
                dve.tensor_tensor(t[0], co, t[8], mul)
                dve.tensor_tensor(t[1], si, t[10], mul)
                dve.tensor_tensor(t[2], co, t[10], mul)
                link(dve.tensor_tensor(t[3], si, t[8], mul))
                dve.tensor_tensor(e[:, 1, :], t[0], t[1], sub)
                link(dve.tensor_tensor(e[:, 2, :], t[2], t[3], add))
                dve.tensor_scalar(e[:, 0, :], e[:, 2, :], -1.0, None, mul).then_inc(roots_done, 1)

            def kernel_columns():
                dve.wait_ge(dft_done, 1)
                y = e[:, 3:5, :].rearrange("p r m -> p (r m)")
                dve.tensor_copy(y, pg[0][:, 0:2 * M8]).then_inc(s4_read, 1)
                dve.wait_ge(s4_read, 2)
                prod = e[:, 5:21, :].rearrange("p a m -> p (a m)").rearrange("p (b i) -> p b i", b=M8)
                link(dve.tensor_tensor(prod, twiddle.rearrange("p (b i) -> p b i", b=M8),
                                       y[:, None, :].broadcast_to((P, M8, 2 * M8)), ALU.mult))
                link(dve.tensor_reduce(kcol[:, :], prod, AX.X, ALU.add))
                dve.tensor_tensor(kcol[0:1, 0:1], kcol[0:1, 0:1], d_sb[:, :], ALU.add).then_inc(kcol_done, 1)

            def kernel_scale():
                dve.wait_ge(kabs_done, 1)
                link(dve.tensor_reduce(kmx[:, :], kabs[:, :], AX.X, ALU.max))
                link(dve.tensor_scalar(ksc[:, 0:1], kmx[:, :].bitcast(i32), 23, None, ALU.logical_shift_right))
                link(dve.tensor_scalar(ksc[:, 0:1], ksc[:, 0:1], 24.0, None, ALU.max))
                dve.tensor_scalar(ksc[:, 1:2], ksc[:, 0:1], -13.0 - XS_LOG, None, ALU.add)
                link(dve.tensor_scalar(ksc[:, 0:1], ksc[:, 0:1], -1.0, 267.0, ALU.mult, ALU.add))
                dve.tensor_scalar(ksc[:, :], ksc[:, :], 23, None, ALU.logical_shift_left).then_inc(kscale_done, 1)

            def first_group():
                x_stats(0)
                x_stats(1)
                w_prep(0, 0, free=False)
                x_stats(2)
                x_low(0)
                x_stats(3)
                for j in range(1, 4):
                    x_low(j)
                w_prep(0, 1, free=False)
                w_prep(0, 2)
                w_prep(0, 3)
                for j in range(4, 8):
                    x_stats(j)
                for b in range(3):
                    for t in range(2):
                        j = 4 * b + 4 + 2 * t
                        x_low(j)
                        x_low(j + 1)
                        h_mult(0, b, t)
                        for i in range(j + 4, min(j + 6, NT)):
                            x_stats(i)
                    if b < 2:
                        w_prep(0, 4 + b)
                accumulate(0, 0)
                w_prep(1, 0)
                accumulate(0, 1)
                w_prep(1, 1)
                h_mult(0, 3, 0)
                w_prep(1, 2)
                h_mult(0, 3, 1)
                w_prep(1, 3)
                accumulate(0, 2)
                w_prep(1, 4)
                w_prep(1, 5)

            def group(g, next_tail=False):
                for b in range(NB):
                    h_mult(g, b, 0)
                    if b == 1:
                        w_prep(g + 1, 1, next_tail)
                    if b == 3 and not next_tail:
                        w_prep(g + 1, 4)
                    h_mult(g, b, 1)
                    if b == 0:
                        accumulate(g - 1, NB - 1)
                    else:
                        accumulate(g, b - 1)
                    if b == 3 and next_tail:
                        tail_down_prep(4)
                        tail_down_prep(5)
                    else:
                        w_prep(g + 1, (0, 2, 3, 5)[b], next_tail)

            def tail_group():
                for b in range(NB):
                    if b == 2:
                        roots()
                    if b == 0:
                        numerators()
                    tail_h_mult(b, 0)
                    if b == 3:
                        kernel_scale()
                    tail_h_mult(b, 1)
                    if b == 0:
                        accumulate(NG - 1, NB - 1)
                        denominators()
                        resolvent()
                    if b == 2:
                        kernel_columns()
                    if b == 3:
                        dve.wait_ge(kt_done, 1)
                        dve.tensor_copy(krow, pg[0][0:M8, 0:P]).then_inc(krow_done, 1)
                    if b >= 1:
                        accumulate(NG, b - 1)
                    if b == 1:
                        cauchy_sums()

            first_group()
            with dve.Fori(0, (LOOP[1] - LOOP[0]) // 2) as it:
                for half_turn in range(2):
                    group(2 * it + (LOOP[0] + half_turn))
            group(NG - 1, next_tail=True)
            tail_group()
            for n in range(2):
                for c in range(2):
                    dve.wait_ge(shi_done, 2 * n + c + 1)
                    dve.scalar_tensor_tensor(out=strip[:, 1, n, c * SB:(c + 1) * SB], in0=(pg, pu)[n][c][:, :],
                                             scalar=ksc[:, 0:1].bitcast(f32), in1=strip[:, 0, n, c * SB:(c + 1) * SB],
                                             op0=ALU.mult, op1=ALU.subtract).then_inc(slo_done, 1)
            accumulate(NG, NB - 1)
            for d in range(2 * NT):
                part = acc[:, d // 2, (d % 2) * SB:(d % 2 + 1) * SB]
                dve.wait_ge(conv_done, d + 1)
                dve.scalar_tensor_tensor(out=part, in0=po[d % 4][:, :], scalar=ksc[:, 1:2].bitcast(f32), in1=part,
                                         op0=ALU.mult, op1=ALU.add).then_inc(conv_added, 1)


def _constants():
    l = np.arange(L)
    ang = np.pi * l / L
    angle = np.stack([np.cos(ang), np.sin(ang)])
    small = np.stack([np.cos(ang).reshape(P, M8), np.sin(ang).reshape(P, M8)], axis=1)
    a = np.arange(P)
    th = 2 * np.pi * np.outer(a, a) / P
    dft = np.stack([np.cos(th), np.sin(th)], axis=1)
    t = a[:, None, None] + P * np.arange(M8)[None, :, None]
    tw = 2 * np.pi * t * np.arange(M8)[None, None, :] / L
    twiddle = np.concatenate([np.cos(tw), -np.sin(tw)], axis=2) / L
    f = np.float32
    return {"ident": np.eye(P, dtype=f), "flip": np.eye(P, dtype=f)[::-1].copy(), "angle": angle.astype(f),
            "small": small.astype(f), "dft": dft.astype(f), "twiddle": twiddle.reshape(P, -1).astype(f)}


def _proj_words(wq):
    t = wq.T.reshape(4, P, I)
    main = t[:, :, :NG * CH].reshape(4, P, NG, P, 2).transpose(2, 1, 0, 4, 3).reshape(NG, P, 4 * CH)
    return main, t[:, :, NG * CH:].reshape(4, P, TAIL, 2)


def _proj_sz(scale, zero):
    t = np.stack([scale.T, zero.T]).reshape(2, 4, 4, I)
    main = t[..., :NG * CH].reshape(2, 4, 4, NG, P, 2).transpose(3, 2, 1, 0, 5, 4).reshape(NG, 4, 8 * CH)
    return main, t[..., NG * CH:].reshape(2, 4, 4, TAIL, 2).transpose(1, 2, 0, 3, 4)


def _tail_tiles(gate, up):
    (ga, gb), (ua, ub) = ((np.concatenate([a[..., 0], a[..., :TA, 1]], axis=-1), a[..., TA:, 1])
                          for a in (gate, up))
    return [np.moveaxis(part, 0, 1).reshape(gate.shape[1], -1)
            for part in (np.concatenate([ga, gb, ub], axis=-1), ua)]


def _down_words(wq):
    t = wq.T
    return t[:NG * P].reshape(NG, P, H), t[NG * P:]


def _down_sz(scale, zero):
    t = np.stack([scale.T, zero.T]).reshape(2, I // GROUP, 2, H // 2)
    main = t[:, :4 * NG].transpose(1, 2, 0, 3).reshape(NG, 4, 2 * H)
    return main, t[:, 4 * NG:].transpose(1, 0, 2, 3).reshape(-1, 2 * H)


def kernel(**inputs):
    import concourse.bacc as _bacc
    from concourse.bass_utils import run_bass_kernel_spmd as _run

    a = {k.replace("L0_attn_", "").replace("L0_ffn_", ""): np.asarray(v) for k, v in inputs.items()}
    rg, tg = _proj_words(a["gate_Wq"])
    ru, tu = _proj_words(a["up_Wq"])
    rd, td = _down_words(a["down_Wq"])
    zg, tzg = _proj_sz(a["gate_scale"], a["gate_zero"])
    zu, tzu = _proj_sz(a["up_scale"], a["up_zero"])
    zd, tzd = _down_sz(a["down_scale"], a["down_zero"])
    tg, tu = _tail_tiles(tg, tu)
    tzg, tzu = _tail_tiles(tzg, tzu)
    arrays = {"x": a["u"].reshape(S, H), "raw_gate": rg, "raw_up": ru, "raw_down": rd,
              "sz_gate": zg, "sz_up": zu, "sz_down": zd,
              "tail_gate": tg, "tail_up": tu, "tail_down": td,
              "tsz_gate": tzg, "tsz_up": tzu, "tsz_down": tzd,
              "lam": a["Lambda_ri"], "p": a["p_ri"], "q": a["q_ri"], "vc": a["Vc_ri"],
              "ct": a["Ct_ri"].reshape(NS, 2), "bp": a["Bp"], "d": a["D"], "ls": a["log_step"]}
    arrays.update(_constants())
    nc = _bacc.Bacc("TRN2", target_bir_lowering=False, num_devices=1)
    feeds, args = {}, []
    for name, arr in arrays.items():
        arr = np.ascontiguousarray(arr)
        feeds[f"in_{name}"] = arr
        args.append(nc.dram_tensor(f"in_{name}", arr.shape, mybir.dt.from_np(arr.dtype), kind="ExternalInput").ap())
    out = nc.dram_tensor("out", (S, H), mybir.dt.float32, kind="ExternalOutput").ap()
    s4_plus_int4_swiglu(nc, *args, out)
    r = _run(nc, [feeds], core_ids=[0])
    return r.results[0]["out"].reshape(1, S, H)
```

```python
import numpy as np
import concourse.bass as bass
from concourse import mybir
from contextlib import ExitStack

S, H, I, NS = 2048, 1024, 2752, 64
P = 128
GROUP = 64
CH = 2 * P
NG = I // CH
TAIL = (I - NG * CH) // 2
TA = P - TAIL
TB = TAIL - TA
SB = 512
NB = S // SB
KC = H // P
NT = S // P
SLAB = 512
L = H
M8 = L // P

XS_LOG = 10
XS, WS, HS = 2.0 ** XS_LOG, 2.0 ** 12, 2.0 ** -2

HALF = SB // 2
A11, A12, A22, S2, S3, S4, S1 = range(7)
B11, B21, B22, T3, T2, T1, T4 = range(7)
PRODUCTS = ((A11, B11, ((1, 0, 0), (1, 1, 0))), (A12, B21, ((1, 0, 0),)), (S4, B22, ((1, 0, 1),)),
            (S2, T2, ((1, 1, 0),)), (S3, T3, ((1, 1, 0), (-1, 0, 1))), (S1, T1, ((1, 1, 1),)),
            (A22, T4, ((1, 1, 0), (-1, 1, 1))))
STEPS = [(i,) + prod for prod in PRODUCTS for i in range(2)]
DB = len(STEPS)
DG = NB * DB
EPS = 1e-5


def s4_plus_int4_swiglu(nc, x_d, raw_gate, raw_up, raw_down, sz_gate, sz_up, sz_down,
                        tail_gate, tail_up, tail_down, tsz_gate, tsz_up, tsz_down,
                        lam_d, p_d, q_d, vc_d, ct_d, bp_d, d_d, ls_d,
                        ident_d, flip_d, angle_d, small_d, dft_d, twiddle_d, out_d):
    f32, f16, i32 = mybir.dt.float32, mybir.dt.float16, mybir.dt.int32
    ALU, ACT, AX = mybir.AluOpType, mybir.ActivationFunctionType, mybir.AxisListType

    ctx = ExitStack()
    with ctx:
        def sb(name, shape, dt=f32):
            return ctx.enter_context(nc.sbuf_tensor(name, shape, dt))

        def sem(name):
            return ctx.enter_context(nc.semaphore(name))

        acc = sb("acc", [P, NT, H])
        xh = sb("xh", [P, KC, S], f16)
        xl = sb("xl", [P, KC, S], f16)
        w_gu = [sb(f"w_gu{i}", [P, 2, 2, KC, CH], f16) for i in range(2)]
        w_dn = sb("w_dn", [P, 2, 7, SB], f16)
        hh = sb("hh", [P, 2, 7, HALF], f16)
        hl = sb("hl", [P, 2, 7, HALF], f16)
        sil = sb("sil", [P, 2, SB])
        hf = sb("hf", [P, 2, SB])
        raw = sb("raw", [P, 2, SLAB], i32)
        sz = sb("sz", [P, 2, 2 * SLAB])
        wf = sb("wf", [P, 2, 2 * SLAB])
        ident = sb("ident", [P, P])
        stats = sb("stats", [P, 2, 2, 6])
        mv = sb("mv", [P, NT, 2])
        negm = sb("negm", [P, NT])
        vs = sb("vs", [P, NT])
        rstd = sb("rstd", [P, NT])
        nmr = sb("nmr", [P, NT])
        half = sb("half", [P, 1])
        par = sb("par", [P, 5, 2])
        vcb = sb("vcb", [P, NS, 2])
        bpb = sb("bpb", [P, NS])
        vw = sb("vw", [P, 8])
        sc = sb("sc", [P, 8])
        d_sb = sb("d_sb", [1, 1])
        cs8 = sb("cs8", [P, 2, M8])
        e = sb("e", [P, 24, M8])
        kcol = sb("kcol", [P, M8])
        zrow = sb("zrow", [1, 2 * P])
        kabs = sb("kabs", [P, M8])
        kmx = sb("kmx", [P, 1])
        ksc = sb("ksc", [P, 2], i32)
        xn = w_gu[1][:, :, :, :, :].rearrange("p a b k c -> p (a b k c)").bitcast(f32)\
            .rearrange("p (j h) -> p j h", j=4)
        s4w = w_gu[1][:, :, :, :, :].rearrange("p a b k c -> p (a b k c)").bitcast(f32)\
            .rearrange("p (j h) -> p j h", j=4)
        strip = w_gu[1][:, 0, :, :, :].rearrange("p b k c -> p b (k c)")\
            .rearrange("p b (n t) -> p b n t", n=2)
        angle = sz
        kshift = wf
        dft = raw[:, 0, 0:2 * P].bitcast(f32).rearrange("p (j a) -> p j a", j=2)
        flip = raw[:, 0, 2 * P:3 * P].bitcast(f32)
        twiddle = raw[:, 1, 0:P].bitcast(f32)
        krow = raw[0:M8, 1, P:2 * P].bitcast(f32)

        pg = [ctx.enter_context(nc.psum_tensor(f"pg{i}", [P, SB], f32)) for i in range(2)]
        pu = [ctx.enter_context(nc.psum_tensor(f"pu{i}", [P, SB], f32)) for i in range(2)]
        po = [ctx.enter_context(nc.psum_tensor(f"po{i}", [P, SB], f32)) for i in range(4)]

        kpad = nc.dram_tensor("kpad", [CH + L], f32, kind="Internal").ap()

        x_in = [sem(f"x_in{j}") for j in range(4 + NB - 1)]
        slab_in = [sem(f"slab_in{j}") for j in range(2)]
        ident_in, par_in, tab_in, kpad_out, kshift_in, out_done = \
            (sem(n) for n in ("ident_in", "par_in", "tab_in", "kpad_out", "kshift_in", "out_done"))
        stat_done, rstd_done, xn_done, xt_done, xhi_done, xlo_done = \
            (sem(n) for n in ("stat_done", "rstd_done", "xn_done", "xt_done", "xhi_done", "xlo_done"))
        gate_done, up_done, down_done, silu_done, hf_done, hhi_done, hlo_done, acc_done = \
            (sem(n) for n in ("gate_done", "up_done", "down_done", "silu_done", "hf_done", "hhi_done",
                              "hlo_done", "acc_done"))
        wprep_done, whi_done, wlo_done, dve_order = \
            (sem(n) for n in ("wprep_done", "whi_done", "wlo_done", "dve_order"))
        dve_order_loop = sem("dve_order_loop")
        hsum_done, wsum_done, encoded, decoded = \
            (sem(n) for n in ("hsum_done", "wsum_done", "encoded", "decoded"))
        step_done, cauchy_done, s4_read, dft_done, krow_done, kzero_done, kt_done = \
            (sem(n) for n in ("step_done", "cauchy_done", "s4_read", "dft_done", "krow_done",
                              "kzero_done", "kt_done"))
        resolvent_done, roots_done, kcol_done, flip_done, shi_done, slo_done = \
            (sem(n) for n in ("resolvent_done", "roots_done", "kcol_done", "flip_done", "shi_done", "slo_done"))
        kabs_done, kscale_done = sem("kabs_done"), sem("kscale_done")
        conv_done, conv_added, pool_order = (sem(n) for n in ("conv_done", "conv_added", "pool_order"))

        def words(k, tail):
            return SLAB // 2 if tail and k in (2, 3) else SLAB

        def sz_view(slot, k, tail):
            w = words(k, tail)
            if k >= 4:
                v = sz[:, slot, 0:2 * w].rearrange("p (z w) -> p z w", z=2)
                return [v[:, z:z + 1, :].broadcast_to((P, 2, w)) for z in range(2)]
            v = sz[:, slot, 0:2 * w].rearrange("p (c z w) -> p c z w", c=2, z=2)
            return [v[:, None, :, z, :].broadcast_to((P, 2, 2, w // 2)) for z in range(2)]

        def wf_view(slot, k, tail, dt=f32):
            w = words(k, tail)
            v = wf[:, slot, 0:2 * w]
            v = v.bitcast(dt) if dt != f32 else v
            if k >= 4:
                return v.rearrange("p (a w) -> p a w", a=2)
            return v.rearrange("p (a c w) -> p a c w", a=2, c=2)

        def w_source(k, tail):
            if k == 5 and not tail:
                return wf[:, 1, SLAB:2 * SLAB]
            w = 2 * words(k, tail)
            return wf[:, (0, 1, 0, 1, 0, 1, 1, 0)[k], 0:w].rearrange("p (c w) -> p c w", c=4 if k < 4 else 2)

        def w_dest(parity, k, part, tail):
            if k >= 4 and tail:
                return w_dn[:, part, 2 * (k - 4):2 * (k - 4) + 2, :]
            if k == 4:
                return w_dn[:, part, B11:B21 + 1, :]
            if k == 5:
                return w_dn[:, part, B22, :]
            if k >= 6:
                return w_dn[:, part, T3 + 2 * (k - 6):T3 + 2 * (k - 6) + 2, :]
            return w_gu[parity][:, k // 2, part, 4 * (k % 2):4 * (k % 2) + 4, 0:words(k, tail) // 2]

        def h_source(i):
            if i == 0:
                return hf[:, 0, 0:HALF]
            return hf[:, i % 2, :].rearrange("p (a s) -> p a s", a=2)

        def h_dest(buf, b, i):
            return buf[:, b % 2, 0, :] if i == 0 else buf[:, b % 2, 2 * i - 1:2 * i + 1, :]

        def tail_h(buf, b, t):
            return buf[:, b % 2, 2 * t:2 * t + 2, :].rearrange("p a s -> p (a s)")

        FIRST = 0
        LOOP = (1, NG - 1)

        block = ctx.enter_context(nc.Block())

        @block.sync
        def _(sp):
            def load_slab(g, k, tail=False, free=True):
                slot = k % 2
                if free:
                    sp.wait_ge(wprep_done, 6 * g + k - 1)
                w = words(k, tail)
                if tail:
                    r = (tail_gate, tail_up)[k // 2][:, (k % 2) * w:(k % 2 + 1) * w]
                    z = (tsz_gate, tsz_up)[k // 2][:, (k % 2) * 2 * w:(k % 2 + 1) * 2 * w]
                else:
                    r = (raw_gate, raw_up, raw_down)[k // 2]
                    z = (sz_gate, sz_up, sz_down)[k // 2]
                    r = r[bass.ds(g, 1), :, (k % 2) * w:(k % 2 + 1) * w].rearrange("g p w -> (g p) w")
                    z = z[bass.ds(g, 1), :, (k % 2) * 2 * w:(k % 2 + 1) * 2 * w].rearrange("g q w -> (g q) w")
                sp.dma_start(raw[:, slot, 0:w], r).then_inc(slab_in[slot], 16)
                sp.dma_start(sz[:, slot, 0:2 * w], z[:, None, :].broadcast_to((4, 32, 2 * w)))\
                    .then_inc(slab_in[slot], 16)

            def load_tail_down(k):
                sp.wait_ge(wprep_done, 6 * NG + k)
                parts = ((0, TAIL, 0), (TAIL, P, 0)) if k == 4 else ((0, TB, TA), (TB, P, TA))
                for p0, p1, row in parts:
                    n = p1 - p0
                    sp.dma_start(raw[p0:p1, :, :].rearrange("p a w -> p (a w)"), tail_down[row:row + n, :])\
                        .then_inc(slab_in[k % 2], 16)
                    z = tsz_down[row // 32:(row + n) // 32, :]
                    sp.dma_start(sz[p0:p1, :, :].rearrange("p a w -> p (a w)"),
                                 z[:, None, :].broadcast_to((n // 32, 32, 2 * H))).then_inc(slab_in[k % 2], 16)

            def load_x(b):
                sp.dma_start(acc[:, 4 * b:4 * b + 4, :],
                             x_d[b * SB:(b + 1) * SB, :].rearrange("(j p) h -> p j h", p=P)).then_inc(x_in[3 + b], 16)

            def load_x_tile(j):
                sp.dma_start(acc[:, j, :], x_d[j * P:(j + 1) * P, :]).then_inc(x_in[j], 16)

            load_x_tile(0)
            load_x_tile(1)
            load_x_tile(2)
            load_x_tile(3)
            load_slab(0, 0, free=False)
            load_slab(0, 1, free=False)
            load_slab(0, 2)
            load_x(1)
            load_slab(0, 3)
            load_x(2)
            load_slab(0, 4)
            load_x(3)
            load_slab(0, 5)
            for h2 in range(2):
                for i, src in enumerate((lam_d, p_d, q_d, ct_d)):
                    sp.dma_start(par[h2 * NS:(h2 + 1) * NS, i, :], src).then_inc(par_in, 16)
                sp.dma_start(vcb[h2 * NS:(h2 + 1) * NS, :, :], vc_d).then_inc(par_in, 16)
            sp.dma_start(bpb[:, :], bp_d.rearrange("n a -> a n").broadcast_to((P, NS))).then_inc(par_in, 16)
            sp.dma_start(sc[:, 0:1], ls_d[:, None].broadcast_to((P, 1))).then_inc(par_in, 16)
            sp.dma_start(d_sb[:, :], d_d[:, None]).then_inc(par_in, 16)
            for k in range(6):
                load_slab(1, k)
            with sp.Fori(0, (LOOP[1] - LOOP[0]) // 2) as it:
                for half_turn in range(2):
                    for k in range(6):
                        load_slab(2 * it + (LOOP[0] + half_turn + 1), k)
            for k in range(4):
                load_slab(NG, k, tail=True)
            load_tail_down(4)
            load_tail_down(5)
            sp.wait_ge(wprep_done, 6 * NG + 6)
            for j in range(2):
                sp.dma_start(angle[:, j, :], angle_d[j:j + 1, :].broadcast_to((P, L))).then_inc(tab_in, 16)
            sp.dma_start(dft, dft_d).then_inc(tab_in, 16)
            sp.dma_start(flip, flip_d).then_inc(tab_in, 16)
            sp.dma_start(twiddle, twiddle_d).then_inc(tab_in, 16)
            sp.dma_start(cs8[:, :, :], small_d).then_inc(tab_in, 16)
            sp.wait_ge(kzero_done, 1)
            sp.dma_start(kpad[0:CH][None, :], zrow[0:1, :]).then_inc(kpad_out, 16)
            sp.wait_ge(krow_done, 1)
            sp.dma_start(kpad[CH:CH + L].rearrange("(b a) -> b a", b=M8), krow).then_inc(kpad_out, 16)
            sp.wait_ge(kpad_out, 32)
            for n in range(2):
                src = bass.AP(kpad.tensor, 2 - n, [[2, P], [1, L]])
                sp.dma_start(kshift[:, n, :], src).then_inc(kshift_in, 16)
            for st in range(NT - 1):
                sp.wait_ge(conv_added, 2 * st + 2)
                sp.dma_start(out_d[st * P:(st + 1) * P, :], acc[:, st, :]).then_inc(out_done, 16)
            for c in range(2):
                sp.wait_ge(conv_added, 2 * NT - 1 + c)
                sp.dma_start(out_d[S - P:S, c * SB:(c + 1) * SB], acc[:, NT - 1, c * SB:(c + 1) * SB])\
                    .then_inc(out_done, 16)
            sp.wait_ge(out_done, 16 * (NT + 1))

        @block.gpsimd
        def _(pool):
            pool.memset(half[:, :], -0.5).then_inc(pool_order, 1)
            pool.memset(zrow[:, :], 0.0).then_inc(kzero_done, 1)
            pool.memset(sc[:, 7:8], float(np.e)).then_inc(pool_order, 1)
            pool.wait_ge(pool_order, 2)

            def x_rstd(j):
                pool.wait_ge(stat_done, j + 1)
                pool.tensor_tensor(rstd[:, j:j + 1], vs[:, j:j + 1], half[:, :], ALU.pow).then_inc(pool_order, 1)
                pool.wait_ge(pool_order, j + 3)
                pool.tensor_tensor(nmr[:, j:j + 1], negm[:, j:j + 1], rstd[:, j:j + 1], ALU.mult)\
                    .then_inc(rstd_done, 1)

            def w_low(g, k, parity, tail=False):
                pool.wait_ge(whi_done, 8 * g + k + 1)
                pool.tensor_tensor(w_dest(parity, k, 1, tail), w_source(k, tail), w_dest(parity, k, 0, tail),
                                   ALU.subtract).then_inc(wlo_done, 1)

            def h_low(g, b, i):
                pool.wait_ge(hhi_done, 16 * g + 4 * b + i + 1)
                pool.tensor_tensor(h_dest(hl, b, i), h_source(i), h_dest(hh, b, i), ALU.subtract)\
                    .then_inc(hlo_done, 1)

            def tail_h_low(b, t):
                r0 = TB if t == 1 else 0
                pool.wait_ge(hlo_done, 16 * NG + 2 * b + t)
                pool.wait_ge(hhi_done, 16 * NG + 2 * b + t + 1)
                pool.tensor_tensor(tail_h(hl, b, t)[r0:P], hf[r0:P, t, :], tail_h(hh, b, t)[r0:P],
                                   ALU.subtract).then_inc(hlo_done, 1)

            def encode(b):
                pool.wait_ge(xn_done, 4 * b + 4)
                first, second = acc[:, 4 * b:4 * b + 2, :], acc[:, 4 * b + 2:4 * b + 4, :]
                pool.tensor_tensor(first[:, :, SB:H], first[:, :, SB:H], second[:, :, SB:H], ALU.subtract)
                pool.tensor_tensor(second[:, :, SB:H], second[:, :, SB:H], second[:, :, 0:SB], ALU.subtract)\
                    .then_inc(encoded, 1)

            def decode(b):
                pool.wait_ge(acc_done, DG * (NG - 1) + DB * (b + 1))
                first, second = acc[:, 4 * b:4 * b + 2, :], acc[:, 4 * b + 2:4 * b + 4, :]
                pool.tensor_tensor(second[:, :, SB:H], second[:, :, SB:H], second[:, :, 0:SB], ALU.add)\
                    .then_inc(decoded, 1)
                pool.wait_ge(decoded, 2 * b + 1)
                pool.tensor_tensor(first[:, :, SB:H], first[:, :, SB:H], second[:, :, SB:H], ALU.add)\
                    .then_inc(decoded, 1)

            def first_group():
                for j in range(4):
                    x_rstd(j)
                w_low(0, 0, 0)
                for k in range(1, 4):
                    w_low(0, k, 0)
                for j in range(4, 8):
                    x_rstd(j)
                h_low(0, 0, 0)
                x_rstd(8)
                h_low(0, 0, 1)
                x_rstd(9)
                w_low(0, 4, 0)
                h_low(0, 0, 2)
                h_low(0, 0, 3)
                x_rstd(10)
                x_rstd(11)
                h_low(0, 1, 0)
                x_rstd(12)
                encode(0)
                h_low(0, 1, 1)
                x_rstd(13)
                encode(1)
                w_low(0, 5, 0)
                h_low(0, 1, 2)
                h_low(0, 1, 3)
                x_rstd(14)
                x_rstd(15)
                w_low(0, 6, 0)
                w_low(0, 7, 0)
                w_low(1, 0, 1)
                w_low(1, 1, 1)
                for i in range(4):
                    h_low(0, 2, i)
                encode(2)
                w_low(1, 2, 1)
                h_low(0, 3, 0)
                h_low(0, 3, 1)
                w_low(1, 3, 1)
                h_low(0, 3, 2)
                h_low(0, 3, 3)
                encode(3)

            def group(g, parity, next_tail=False):
                for b in range(NB):
                    h_low(g, b, 0)
                    if b >= 2:
                        w_low(g + 1, 2 * b - 3, 1 - parity, next_tail)
                    h_low(g, b, 1)
                    if b == 0:
                        w_low(g, 4, parity)
                        w_low(g, 5, parity)
                    h_low(g, b, 2)
                    h_low(g, b, 3)
                    if b == 0:
                        w_low(g, 6, parity)
                        w_low(g, 7, parity)
                    if b in (1, 2):
                        w_low(g + 1, 2 * b - 2, 1 - parity, next_tail)

            def tail_group(parity):
                for b in range(3):
                    decode(b)
                for b in range(NB):
                    tail_h_low(b, 0)
                    tail_h_low(b, 1)
                    pool.wait_ge(hlo_done, 16 * NG + 2 * b + 2)
                    if b == 0:
                        w_low(NG, 4, parity, True)
                        w_low(NG, 5, parity, True)
                        decode(3)
                    if b == 2:
                        pool.wait_ge(kcol_done, 1)
                        pool.partition_all_reduce(kabs[:, :], kcol[:, :], P, bass.bass_isa.ReduceOp.absmax)\
                            .then_inc(kabs_done, 1)

            first_group()
            pool.wait_ge(par_in, 16 * 13)
            pool.tensor_tensor(sc[:, 1:2], sc[:, 7:8], sc[:, 0:1], ALU.pow).then_inc(step_done, 1)
            with pool.Fori(0, (LOOP[1] - LOOP[0]) // 2) as it:
                for half_turn in range(2):
                    group(2 * it + (LOOP[0] + half_turn), (LOOP[0] + half_turn) % 2)
            group(NG - 1, (NG - 1) % 2, next_tail=True)
            tail_group(NG % 2)

        @block.scalar
        def _(act):
            act.dma_start(ident[:, :], ident_d).then_inc(ident_in, 16)

            def normalize(j):
                act.wait_ge(rstd_done, j + 1)
                act.wait_ge(x_in[min(j, 3 + j // 4)], 16)
                if j >= 4:
                    act.wait_ge(xt_done, 2 * j - 6)
                act.activation(xn[:, j % 4, :], acc[:, j, :], ACT.Identity, scale=rstd[:, j:j + 1],
                               bias=nmr[:, j:j + 1]).then_inc(xn_done, 1)

            def x_high(j):
                for hf2 in range(2):
                    act.wait_ge(xt_done, 2 * j + hf2 + 1)
                    act.activation(xh[:, 4 * hf2:4 * hf2 + 4, j * P:(j + 1) * P],
                                   po[2 * (j % 2) + hf2][:, :].rearrange("p (k s) -> p k s", k=4),
                                   ACT.Copy).then_inc(xhi_done, 1)

            def w_high(g, k, parity, tail=False):
                if k < 6:
                    act.wait_ge(wprep_done, 6 * g + k + 1)
                else:
                    act.wait_ge(wsum_done, 3 * g + k - 4)
                if g is not FIRST:
                    if k < 4:
                        act.wait_ge(up_done, 8 * g - 8)
                    elif k < 6:
                        act.wait_ge(down_done, DG * g)
                act.activation(w_dest(parity, k, 0, tail), w_source(k, tail), ACT.Copy).then_inc(whi_done, 1)

            def silu(g, b, t, tail):
                idx = 8 * g + 2 * b + t
                act.wait_ge(gate_done, idx + 1)
                if not (g is FIRST and b == 0):
                    act.wait_ge(hf_done, idx - 1)
                if tail and t == 1:
                    out, gate = sil[TB:P, t, :], pg[t][0:TB, :]
                else:
                    out, gate = sil[:, t, :], pg[t][:, :]
                act.activation(out, gate, ACT.Silu, scale=1.0 / (XS * WS)).then_inc(silu_done, 1)

            def h_high(g, b, i):
                if i < 2:
                    act.wait_ge(hf_done, 8 * g + 2 * b + i + 1)
                    if not (g is FIRST and b < 2):
                        act.wait_ge(down_done, DG * g + DB * b - DB)
                else:
                    act.wait_ge(hsum_done, 12 * g + 3 * b + i)
                act.activation(h_dest(hh, b, i), h_source(i), ACT.Copy).then_inc(hhi_done, 1)

            def tail_h_high(b, t):
                act.wait_ge(hf_done, 8 * NG + 2 * b + t + 1)
                act.wait_ge(down_done, DG * NG + (8 if b >= 2 else DB) * (b - 1))
                if t == 1:
                    act.activation(tail_h(hl, b, t)[0:TB], hf[TB:P, t, :], ACT.Copy)
                    act.activation(tail_h(hh, b, t)[TB:P], hf[TB:P, t, :], ACT.Copy).then_inc(hhi_done, 1)
                else:
                    act.activation(tail_h(hh, b, t), hf[:, t, :], ACT.Copy).then_inc(hhi_done, 1)

            def first_group():
                for j in (0, 1):
                    normalize(j)
                x_high(0)
                normalize(2)
                normalize(3)
                x_high(1)
                w_high(0, 0, 0)
                x_high(2)
                x_high(3)
                for k in range(1, 4):
                    w_high(0, k, 0)
                normalize(4)
                normalize(5)
                for b in range(3):
                    for t in range(2):
                        j = 4 * b + 4 + 2 * t
                        if t == 0 or b < 2:
                            normalize(j + 2)
                        x_high(j)
                        x_high(j + 1)
                        if b == 2 and t == 0:
                            w_high(0, 6, 0)
                            w_high(0, 7, 0)
                        silu(0, b, t, False)
                        if t == 0:
                            normalize(j + 3)
                        if b < 2:
                            h_high(0, b, t)
                        if t == 1 and b < 2:
                            normalize(j + 3)
                            w_high(0, 4 + b, 0)
                            h_high(0, b, 2)
                            h_high(0, b, 3)
                act.wait_ge(xt_done, 2 * NT)
                w_high(1, 0, 1)
                w_high(1, 1, 1)
                for i in range(4):
                    h_high(0, 2, i)
                silu(0, 3, 0, False)
                w_high(1, 2, 1)
                h_high(0, 3, 0)
                silu(0, 3, 1, False)
                h_high(0, 3, 1)
                w_high(1, 3, 1)
                h_high(0, 3, 2)
                h_high(0, 3, 3)

            def group(g, parity, next_tail=False):
                for b in range(NB):
                    silu(g, b, 0, False)
                    h_high(g, b, 0)
                    if b >= 2:
                        w_high(g + 1, 2 * b - 3, 1 - parity, next_tail)
                    silu(g, b, 1, False)
                    h_high(g, b, 1)
                    if b == 0:
                        w_high(g, 4, parity)
                        w_high(g, 5, parity)
                    h_high(g, b, 2)
                    h_high(g, b, 3)
                    if b == 0:
                        w_high(g, 6, parity)
                        w_high(g, 7, parity)
                    if b in (1, 2):
                        w_high(g + 1, 2 * b - 2, 1 - parity, next_tail)

            def tail_group(parity):
                for b in range(NB):
                    for t in range(2):
                        silu(NG, b, t, True)
                        tail_h_high(b, t)
                    if b == 0:
                        w_high(NG, 4, parity, True)
                        w_high(NG, 5, parity, True)

            first_group()
            with act.Fori(0, (LOOP[1] - LOOP[0]) // 2) as it:
                for half_turn in range(2):
                    group(2 * it + (LOOP[0] + half_turn), (LOOP[0] + half_turn) % 2)
            group(NG - 1, (NG - 1) % 2, next_tail=True)
            tail_group(NG % 2)
            act.wait_ge(kscale_done, 1)
            for n in range(2):
                for c in range(2):
                    act.wait_ge(flip_done, 2 * n + c + 1)
                    act.activation(strip[:, 0, n, c * SB:(c + 1) * SB], (pg, pu)[n][c][:, :], ACT.Copy,
                                   scale=ksc[:, 0:1].bitcast(f32)).then_inc(shi_done, 1)

        @block.tensor
        def _(pe):
            pe.wait_ge(ident_in, 16)

            def x_transpose(j):
                pe.wait_ge(xn_done, j + 1)
                for hf2 in range(2):
                    if j >= 2:
                        pe.wait_ge(xlo_done, 2 * j + hf2 - 3)
                    for kk in range(4):
                        first_h = 2 * P * (2 * hf2 + kk % 2) + kk // 2
                        last = pe.transpose(po[2 * (j % 2) + hf2][:, kk * P:(kk + 1) * P],
                                            xn[:, j % 4, first_h:first_h + 2 * P - 1:2], ident[:, :])
                    last.then_inc(xt_done, 1)

            def project(g, b, t, mat, parity, first, k0=0, k1=KC):
                idx = 8 * g + 2 * b + t
                bank = (pg, pu)[mat][t]
                if not (first and b == 0):
                    pe.wait_ge((silu_done, hf_done)[mat], idx - 1)
                w = w_gu[parity]
                toks = slice(b * SB, (b + 1) * SB)
                for k in range(k0, k1):
                    if first and b == 0 and t == 0 and k % 4 == 0:
                        pe.wait_ge(wlo_done, 2 * mat + k // 4 + 1)
                    for wp, xp in ((0, xh), (0, xl), (1, xh)):
                        last = pe.matmul(bank[:, :], w[:, mat, wp, k, t * P:(t + 1) * P], xp[:, k, toks],
                                         start=(k == 0 and wp == 0 and xp is xh), stop=(k == KC - 1 and wp == 1))
                if k1 == KC:
                    last.then_inc((gate_done, up_done)[mat], 1)

            def down(g, b, n0, n1, first=False):
                for n in range(n0, n1):
                    i, ha, wb, _targets = STEPS[n]
                    if n == 0:
                        pe.wait_ge(hlo_done, 16 * g + 4 * b + 2)
                    if n == 4:
                        pe.wait_ge(hlo_done, 16 * g + 4 * b + 4)
                    if b == 0 and n in (0, 4, 6):
                        pe.wait_ge(wlo_done, 8 * g + {0: 5, 4: 6, 6: 8}[n])
                    if not (first and b == 0 and n < 4):
                        pe.wait_ge(acc_done, DG * g + DB * b + n - 3)
                    for hp, wp in ((hh, 0), (hh, 1), (hl, 0)):
                        last = pe.matmul(po[(DB * b + n) % 4][:, :], hp[:, b % 2, ha, i * P:(i + 1) * P],
                                         w_dn[:, wp, wb, :], start=(hp is hh and wp == 0), stop=(hp is hl))
                    last.then_inc(down_done, 1)

            def tail_down(b):
                pe.wait_ge(hlo_done, 16 * NG + 2 * b + 2)
                for d in range(8):
                    st, hd = d // 2, d % 2
                    pe.wait_ge(acc_done, DG * NG + 8 * b + d - 3)
                    steps = [(0, hh, P, 0), (0, hh, P, 1), (0, hl, P, 0), (1, hl, P, 0), (1, hl, TB, 1)]
                    for i, (t, hp, n, wp) in enumerate(steps):
                        last = pe.matmul(po[d % 4][:, :], tail_h(hp, b, t)[0:n, st * P:(st + 1) * P],
                                         w_dn[0:n, wp, 2 * t + hd, :], start=(i == 0), stop=(i == len(steps) - 1))
                    last.then_inc(down_done, 1)

            def tail_project(b, piece, parity):
                t = piece // 2
                if piece == 1:
                    bank, mat = pu[b % 2], 1
                    pe.wait_ge(hf_done, 8 * NG + max(2 * b - 2, b - 1))
                else:
                    bank, mat = pg[t], 0
                    pe.wait_ge(hf_done, 8 * NG + 2 * b + t - 1)
                for k in range(KC):
                    for wp, xp in ((0, xh), (0, xl), (1, xh)):
                        last = pe.matmul(bank[:, :], w_gu[parity][:, mat, wp, k, t * P:(t + 1) * P],
                                         xp[:, k, b * SB:(b + 1) * SB],
                                         start=(k == 0 and wp == 0 and xp is xh), stop=(k == KC - 1 and wp == 1))
                last.then_inc((gate_done, up_done)[mat], 1)

            def group(g, parity):
                for b in range(NB):
                    before = (g - 1, NB - 1) if b == 0 else (g, b - 1)
                    cut = (5, DB) if b == 0 else (4, 9)
                    for t in range(2):
                        for mat in range(2):
                            if b == 0 and t == 0:
                                pe.wait_ge(wlo_done, 8 * g + 2 + 2 * mat)
                            project(g, b, t, mat, parity, False)
                            if t == 1 or mat == 1:
                                down(*before, (0, *cut)[2 * t + mat - 1], (*cut, DB)[2 * t + mat - 1])

            def first_group():
                for j in range(4):
                    x_transpose(j)
                half_k = KC // 2
                for b in range(NB - 1):
                    pe.wait_ge(xlo_done, 8 * b + 8)
                    if b == 0:
                        for k in (0, half_k):
                            for t in range(2):
                                project(0, 0, t, 0, 0, True, k, k + half_k)
                    else:
                        project(0, b, 0, 0, 0, True)
                    project(0, b, 0, 1, 0, True)
                    x_transpose(4 * b + 4)
                    x_transpose(4 * b + 5)
                    if b == 0:
                        project(0, 0, 1, 1, 0, True, 0, 2)
                    else:
                        project(0, b, 1, 0, 0, True)
                    x_transpose(4 * b + 6)
                    x_transpose(4 * b + 7)
                    project(0, b, 1, 1, 0, True, 2 if b == 0 else 0)
                pe.wait_ge(xlo_done, 2 * NT)
                for t in range(2):
                    for mat in range(2):
                        down(0, t, mat * DB // 2, (mat + 1) * DB // 2, first=True)
                        project(0, 3, t, mat, 0, True)
                down(0, 2, 0, DB)

            def tail_group(parity):
                for b in range(NB):
                    for piece in range(3):
                        if b == 0:
                            pe.wait_ge(wlo_done, 8 * NG + 2 + 2 * min(piece, 1))
                        if b >= 2 and piece == 4 - 2 * (b - 1):
                            pe.wait_ge(s4_read, b - 1)
                        tail_project(b, piece, parity)
                        if b == 0 and piece > 0:
                            down(NG - 1, NB - 1, (piece - 1) * DB // 2, piece * DB // 2)
                    if b >= 2:
                        s4_steps(b)
                    if b >= 1:
                        if b == 1:
                            pe.wait_ge(wlo_done, 8 * NG + 6)
                        tail_down(b - 1)
                    if b == 1:
                        s4_steps(b)

            def s4_steps(b):
                if b == 1:
                    pe.wait_ge(resolvent_done, 1)
                    pe.wait_ge(hf_done, 8 * NG + 4)
                    for m in range(M8):
                        last = pe.matmul(pg[1][:, 8 * m:8 * m + 8], s4w[:, 2, m:L:M8], vw[:, :],
                                         start=True, stop=True)
                    last.then_inc(cauchy_done, 1)
                if b == 2:
                    pe.wait_ge(roots_done, 1)
                    pe.wait_ge(hf_done, 8 * NG + 5)
                    pe.matmul(pg[0][:, 0:2 * M8], dft[:, 0, :], e[:, 1:3, :], start=True, stop=False)
                    pe.matmul(pg[0][:, 0:2 * M8], dft[:, 1, :], e[:, 0:2, :], start=False, stop=True)\
                        .then_inc(dft_done, 1)
                if b == 3:
                    pe.wait_ge(kcol_done, 1)
                    pe.wait_ge(hf_done, 8 * NG + 7)
                    pe.transpose(pg[0][0:M8, 0:P], kcol[:, :], ident[:, :]).then_inc(kt_done, 1)

            first_group()
            with pe.Fori(0, (LOOP[1] - LOOP[0]) // 2) as it:
                for half_turn in range(2):
                    group(2 * it + (LOOP[0] + half_turn), (LOOP[0] + half_turn) % 2)
            group(NG - 1, (NG - 1) % 2)
            tail_group(NG % 2)
            pe.wait_ge(kshift_in, 32)
            pe.wait_ge(hf_done, 8 * NG + 8)
            pe.wait_ge(krow_done, 1)
            for n in range(2):
                for c in range(2):
                    pe.matmul((pg, pu)[n][c][:, :], flip, kshift[:, n, c * SB:(c + 1) * SB],
                              start=True, stop=True).then_inc(flip_done, 1)
            tail_down(NB - 1)
            pe.wait_ge(slo_done, 4)
            for st in range(NT):
                for c in range(2):
                    d = 2 * st + c
                    pe.wait_ge(acc_done, DG * NG + 8 * NB - 3 + min(d, 3))
                    if d >= 4:
                        pe.wait_ge(conv_added, d - 3)
                    chunks = [k for k in range(KC) if 2 * P * (2 * (k // 4) + k % 2) < (c + 1) * SB]
                    for k in chunks:
                        h0, nib = 2 * P * (2 * (k // 4) + k % 2), (k // 2) % 2
                        t0 = max(c * SB, h0)
                        for xp, sp_ in ((xh, 0), (xh, 1), (xl, 0)):
                            last = pe.matmul(po[d % 4][:, t0 - c * SB:SB], xp[:, k, st * P:(st + 1) * P],
                                             strip[:, sp_, nib, t0 - h0:(c + 1) * SB - h0],
                                             start=(k == 0 and xp is xh and sp_ == 0),
                                             stop=(k == chunks[-1] and xp is xl))
                    last.then_inc(conv_done, 1)

        @block.vector
        def _(dve):
            chain = [0]

            def link(ins):
                chain[0] += 1
                ins.then_inc(dve_order, 1)
                dve.wait_ge(dve_order, chain[0])

            def x_stats(j):
                dve.wait_ge(x_in[min(j, 3 + j // 4)], 16)
                for c in range(2):
                    last = dve.bn_stats(stats[:, j % 2, c, :], acc[:, j, c * SB:(c + 1) * SB])
                link(last)
                link(dve.bn_aggr(mv[:, j, :], stats[:, j % 2, :, :].rearrange("p c s -> p (c s)")))
                link(dve.tensor_scalar(negm[:, j:j + 1], mv[:, j, 0:1], -1.0, None, ALU.mult))
                dve.tensor_scalar(vs[:, j:j + 1], mv[:, j, 1:2], XS ** -2, EPS * XS ** -2, ALU.mult, ALU.add)\
                    .then_inc(stat_done, 1)

            def x_low(j):
                for hf2 in range(2):
                    dst = (slice(None), slice(4 * hf2, 4 * hf2 + 4), slice(j * P, (j + 1) * P))
                    dve.wait_ge(xhi_done, 2 * j + hf2 + 1)
                    dve.tensor_tensor(xl[dst], po[2 * (j % 2) + hf2][:, :].rearrange("p (k s) -> p k s", k=4),
                                      xh[dst], ALU.subtract).then_inc(xlo_done, 1)

            def tail_down_prep(k):
                slot, n = k % 2, 6 * NG + k
                dve.wait_ge(slab_in[slot], 96 * NG + 64 + 64)
                dve.wait_ge(wlo_done, 8 * NG + k - 1)
                r = raw[:, :, :].rearrange("p a w -> p (a w)")
                q, w = wf[:, slot, :].bitcast(i32), wf[:, slot, :]
                z = sz[:, :, :]
                if k == 4:
                    dve.tensor_scalar(q[0:TAIL], r[0:TAIL], 4, 15, ALU.arith_shift_right, ALU.bitwise_and)
                    last = dve.tensor_scalar(q[TAIL:P], r[TAIL:P], 15, None, ALU.bitwise_and)
                else:
                    last = dve.tensor_scalar(q, r, 15, None, ALU.bitwise_and)
                last.then_inc(dve_order_loop, 1)
                dve.wait_ge(dve_order_loop, 2 * n + 1)
                dve.tensor_tensor(w, q, z[:, 1, :], ALU.subtract).then_inc(dve_order_loop, 1)
                dve.wait_ge(dve_order_loop, 2 * n + 2)
                dve.scalar_tensor_tensor(out=w, in0=w, scalar=WS, in1=z[:, 0, :], op0=ALU.mult, op1=ALU.mult)\
                    .then_inc(wprep_done, 1)

            def w_prep(g, k, tail=False, free=True):
                slot, n = k % 2, 6 * g + k
                dve.wait_ge(slab_in[slot], 32 * 3 * g + 32 * (k // 2 + 1))
                if free:
                    dve.wait_ge(wlo_done, 8 * g + (k - 1 if k >= 2 else -k))
                q = wf_view(slot, k, tail, i32)
                w = wf_view(slot, k, tail)
                r = raw[:, slot, 0:words(k, tail)]
                if k < 4:
                    r = r.rearrange("p (c w) -> p c w", c=2)
                scale, zero = sz_view(slot, k, tail)
                dve.tensor_scalar(q[:, 0], r, 4, 15, ALU.arith_shift_right, ALU.bitwise_and)
                dve.tensor_scalar(q[:, 1], r, 15, None, ALU.bitwise_and).then_inc(dve_order_loop, 1)
                dve.wait_ge(dve_order_loop, 2 * n + 1)
                dve.tensor_tensor(w, q, zero, ALU.subtract).then_inc(dve_order_loop, 1)
                dve.wait_ge(dve_order_loop, 2 * n + 2)
                for nib in range(2):
                    last = dve.scalar_tensor_tensor(out=w[:, nib], in0=w[:, nib], scalar=WS, in1=scale[:, nib],
                                                    op0=ALU.mult, op1=ALU.mult)
                last.then_inc(wprep_done, 1)

            def tail_h_mult(b, t):
                if t == 0:
                    dve.wait_ge(up_done, 8 * NG + b + 1)
                dve.wait_ge(silu_done, 8 * NG + 2 * b + t + 1)
                dve.wait_ge(hlo_done, 16 * NG + 2 * b + t - 1)
                r0, up = ((0, pu[b % 2][:, :]), (TB, pg[1][TB:P, :]))[t]
                dve.scalar_tensor_tensor(out=hf[r0:P, t, :], in0=up, scalar=HS / (XS * WS),
                                         in1=sil[r0:P, t, :], op0=ALU.mult, op1=ALU.mult).then_inc(hf_done, 1)

            def h_mult(g, b, t):
                idx = 8 * g + 2 * b + t
                dve.wait_ge(up_done, idx + 1)
                dve.wait_ge(silu_done, idx + 1)
                if not (g is FIRST and b == 0):
                    dve.wait_ge(hlo_done, 16 * g + 4 * b - 1 + t)
                dve.scalar_tensor_tensor(out=hf[:, t, :], in0=pu[t][:, :], scalar=HS / (XS * WS),
                                         in1=sil[:, t, :], op0=ALU.mult, op1=ALU.mult).then_inc(hf_done, 1)

            def h_sums(g, b):
                a11, a21, a12, a22 = (hf[:, t, p * HALF:(p + 1) * HALF] for t in range(2) for p in range(2))
                s2, s3, s4, s1 = a11, a21, a12, a22
                dve.wait_ge(hlo_done, 16 * g + 4 * b + 2)
                dve.tensor_tensor(s1, a21, a22, ALU.add)
                dve.tensor_tensor(s3, a11, a21, ALU.subtract).then_inc(hsum_done, 1)
                dve.wait_ge(hsum_done, 12 * g + 3 * b + 1)
                dve.tensor_tensor(s2, s1, a11, ALU.subtract).then_inc(hsum_done, 1)
                dve.wait_ge(hsum_done, 12 * g + 3 * b + 2)
                dve.tensor_tensor(s4, a12, s2, ALU.subtract).then_inc(hsum_done, 1)

            def w_sums(g):
                b11, b21, b12, b22 = (wf[:, j, i * SLAB:(i + 1) * SLAB] for j in range(2) for i in range(2))
                t1, t4, t3, t2 = b11, b21, b12, b22
                dve.wait_ge(wlo_done, 8 * g + 6)
                dve.tensor_tensor(t1, b12, b11, ALU.subtract)
                dve.tensor_tensor(t3, b22, b12, ALU.subtract).then_inc(wsum_done, 1)
                dve.wait_ge(wsum_done, 3 * g + 1)
                dve.tensor_tensor(t2, b22, t1, ALU.subtract).then_inc(wsum_done, 1)
                dve.wait_ge(wsum_done, 3 * g + 2)
                dve.tensor_tensor(t4, b21, t2, ALU.subtract).then_inc(wsum_done, 1)

            def accumulate(g, b, n0, n1):
                if g is FIRST and n0 == 0:
                    dve.wait_ge(encoded, b + 1)
                for n in range(n0, n1):
                    i, _a, _b, targets = STEPS[n]
                    dve.wait_ge(down_done, DG * g + DB * b + n + 1)
                    if n >= 2:
                        dve.wait_ge(acc_done, DG * g + DB * b + n - 1)
                    for sign, p, hd in targets:
                        part = acc[:, 4 * b + 2 * p + i, hd * SB:(hd + 1) * SB]
                        last = dve.scalar_tensor_tensor(out=part, in0=po[(DB * b + n) % 4][:, :],
                                                        scalar=sign / (WS * HS), in1=part,
                                                        op0=ALU.mult, op1=ALU.add)
                    last.then_inc(acc_done, 1)

            def tail_accumulate(b):
                dve.wait_ge(decoded, 2 * b + 2)
                for d in range(8):
                    part = acc[:, 4 * b + d // 2, (d % 2) * SB:(d % 2 + 1) * SB]
                    dve.wait_ge(down_done, DG * NG + 8 * b + d + 1)
                    dve.scalar_tensor_tensor(out=part, in0=po[d % 4][:, :], scalar=1.0 / (WS * HS), in1=part,
                                             op0=ALU.mult, op1=ALU.add).then_inc(acc_done, 1)

            def numerators():
                dve.wait_ge(par_in, 16 * 13)
                dve.wait_ge(step_done, 1)
                t3 = e[:, 0:16, :].rearrange("p a m -> p (a m)").rearrange("p (r n) -> p r n", r=2)
                link(dve.tensor_tensor(t3, vcb[:, :, :].rearrange("p n r -> p r n"),
                                       bpb[:, None, :].broadcast_to((P, 2, NS)), ALU.mult))
                link(dve.tensor_reduce(par[:, 4, :], t3, AX.X, ALU.add))
                ar = e[:, 16, 0:2]
                ai = e[:, 16, 2:4]
                br = e[:, 16, 4:6]
                bi = e[:, 16, 6:8]
                for dst, src in ((ar, (3, 2)), (br, (4, 1))):
                    for j in range(2):
                        dve.tensor_copy(dst[:, j:j + 1], par[:, src[j], 0:1])
                for dst, src in ((ai, (3, 2)), (bi, (4, 1))):
                    for j in range(2):
                        last = dve.tensor_copy(dst[:, j:j + 1], par[:, src[j], 1:2])
                link(last)

                def outer(a, b_):
                    return a[:, :, None].broadcast_to((P, 2, 2)), b_[:, None, :].broadcast_to((P, 2, 2))

                m = [e[:, 17 + j // 2, 4 * (j % 2):4 * (j % 2) + 4].rearrange("p (a b) -> p a b", a=2)
                     for j in range(4)]
                for o, (a, b_) in zip(m, ((ar, br), (ai, bi), (ar, bi), (ai, br))):
                    i0, i1 = outer(a, b_)
                    last = dve.tensor_tensor(o, i0, i1, ALU.mult)
                link(last)
                v = [e[:, 19, 4 * j:4 * j + 4].rearrange("p (a b) -> p a b", a=2) for j in range(2)]
                dve.tensor_tensor(v[0], m[0], m[1], ALU.add)
                link(dve.tensor_tensor(v[1], m[2], m[3], ALU.subtract))
                dve.tensor_copy(vw[0:NS, :], e[0:NS, 19, :])
                dve.tensor_scalar(vw[NS:P, 0:4], e[NS:P, 19, 4:8], -1.0, None, ALU.mult)
                dve.tensor_copy(vw[NS:P, 4:8], e[NS:P, 19, 0:4])
                link(dve.reciprocal(sc[:, 2:3], sc[:, 1:2]))
                link(dve.tensor_scalar(sc[:, 2:3], sc[:, 2:3], 2.0, None, ALU.mult))
                dve.tensor_scalar(sc[:, 3:5], par[:, 0, :], -1.0, None, ALU.mult)
                dve.tensor_scalar(sc[0:NS, 5:6], par[0:NS, 0, 0:1], -1.0, None, ALU.mult)
                dve.tensor_copy(sc[NS:P, 5:6], par[NS:P, 0, 1:2])
                dve.memset(sc[0:NS, 6:7], 0.0)
                link(dve.tensor_scalar(sc[NS:P, 6:7], sc[NS:P, 2:3], -1.0, None, ALU.mult))

            def denominators():
                dve.wait_ge(tab_in, 16 * 6)
                dve.wait_ge(up_done, 8 * NG)
                re, im, res = s4w[:, 0, :], s4w[:, 1, :], s4w[:, 2, :]
                dve.tensor_scalar(re, angle[:, 0, :], sc[:, 3:4], None, ALU.mult)
                dve.tensor_scalar(im, angle[:, 1, :], sc[:, 2:3], None, ALU.mult)
                link(dve.tensor_scalar(res, angle[:, 0, :], sc[:, 5:6], None, ALU.mult))
                dve.scalar_tensor_tensor(out=im, in0=angle[:, 0, :], scalar=sc[:, 4:5], in1=im,
                                         op0=ALU.mult, op1=ALU.add)
                link(dve.scalar_tensor_tensor(out=res, in0=angle[:, 1, :], scalar=sc[:, 6:7], in1=res,
                                              op0=ALU.mult, op1=ALU.add))
                dve.tensor_tensor(re, re, re, ALU.mult)
                link(dve.tensor_tensor(im, im, im, ALU.mult))
                link(dve.tensor_tensor(re, re, im, ALU.add))

            def resolvent():
                re, res = s4w[:, 0, :], s4w[:, 2, :]
                link(dve.reciprocal(re, re))
                dve.tensor_tensor(res, res, re, ALU.mult).then_inc(resolvent_done, 1)

            def cauchy_sums():
                dve.wait_ge(cauchy_done, 1)
                sums = pg[1][:, 0:8 * M8].rearrange("p (m j) -> p j m", j=8)
                dve.tensor_copy(e[:, 3:11, :], sums).then_inc(s4_read, 1)

            def roots():
                dve.wait_ge(s4_read, 1)
                r00, r01, r10, r11, i00, i01, i10, i11 = (e[:, 3 + j, :] for j in range(8))
                co, si = cs8[:, 0, :], cs8[:, 1, :]
                t = [e[:, 11 + j, :] for j in range(13)]
                mul, add, sub = ALU.mult, ALU.add, ALU.subtract
                dve.tensor_tensor(t[0], r01, r10, mul)
                dve.tensor_tensor(t[1], i01, i10, mul)
                dve.tensor_tensor(t[2], r01, i10, mul)
                dve.tensor_tensor(t[3], i01, r10, mul)
                dve.tensor_tensor(t[4], co, r11, mul)
                link(dve.tensor_tensor(t[5], co, i11, mul))
                dve.tensor_tensor(t[0], t[0], t[1], sub)
                dve.tensor_tensor(t[2], t[2], t[3], add)
                link(dve.tensor_scalar(t[4], t[4], 1.0, None, add))
                dve.tensor_tensor(t[6], t[4], t[4], mul)
                link(dve.tensor_tensor(t[7], t[5], t[5], mul))
                link(dve.tensor_tensor(t[6], t[6], t[7], add))
                link(dve.reciprocal(t[6], t[6]))
                link(dve.tensor_tensor(t[6], t[6], co, mul))
                dve.tensor_tensor(t[8], t[0], t[4], mul)
                dve.tensor_tensor(t[9], t[2], t[5], mul)
                dve.tensor_tensor(t[10], t[2], t[4], mul)
                link(dve.tensor_tensor(t[11], t[0], t[5], mul))
                dve.tensor_tensor(t[8], t[8], t[9], add)
                link(dve.tensor_tensor(t[10], t[10], t[11], sub))
                dve.tensor_tensor(t[8], t[8], t[6], mul)
                link(dve.tensor_tensor(t[10], t[10], t[6], mul))
                dve.tensor_tensor(t[8], r00, t[8], sub)
                link(dve.tensor_tensor(t[10], i00, t[10], sub))
                dve.tensor_tensor(t[0], co, t[8], mul)
                dve.tensor_tensor(t[1], si, t[10], mul)
                dve.tensor_tensor(t[2], co, t[10], mul)
                link(dve.tensor_tensor(t[3], si, t[8], mul))
                dve.tensor_tensor(e[:, 1, :], t[0], t[1], sub)
                link(dve.tensor_tensor(e[:, 2, :], t[2], t[3], add))
                dve.tensor_scalar(e[:, 0, :], e[:, 2, :], -1.0, None, mul).then_inc(roots_done, 1)

            def kernel_columns():
                dve.wait_ge(dft_done, 1)
                y = e[:, 3:5, :].rearrange("p r m -> p (r m)")
                dve.tensor_copy(y, pg[0][:, 0:2 * M8]).then_inc(s4_read, 1)
                dve.wait_ge(s4_read, 2)
                prod = e[:, 5:21, :].rearrange("p a m -> p (a m)").rearrange("p (b i) -> p b i", b=M8)
                link(dve.tensor_tensor(prod, twiddle.rearrange("p (b i) -> p b i", b=M8),
                                       y[:, None, :].broadcast_to((P, M8, 2 * M8)), ALU.mult))
                link(dve.tensor_reduce(kcol[:, :], prod, AX.X, ALU.add))
                dve.tensor_tensor(kcol[0:1, 0:1], kcol[0:1, 0:1], d_sb[:, :], ALU.add).then_inc(kcol_done, 1)

            def kernel_scale():
                dve.wait_ge(kabs_done, 1)
                link(dve.tensor_reduce(kmx[:, :], kabs[:, :], AX.X, ALU.max))
                link(dve.tensor_scalar(ksc[:, 0:1], kmx[:, :].bitcast(i32), 23, None, ALU.logical_shift_right))
                link(dve.tensor_scalar(ksc[:, 0:1], ksc[:, 0:1], 24.0, None, ALU.max))
                dve.tensor_scalar(ksc[:, 1:2], ksc[:, 0:1], -13.0 - XS_LOG, None, ALU.add)
                link(dve.tensor_scalar(ksc[:, 0:1], ksc[:, 0:1], -1.0, 267.0, ALU.mult, ALU.add))
                dve.tensor_scalar(ksc[:, :], ksc[:, :], 23, None, ALU.logical_shift_left).then_inc(kscale_done, 1)

            def first_group():
                x_stats(0)
                x_stats(1)
                x_stats(2)
                x_stats(3)
                x_low(0)
                w_prep(0, 0, free=False)
                for j in range(1, 4):
                    x_low(j)
                w_prep(0, 1, free=False)
                w_prep(0, 2)
                w_prep(0, 3)
                for j in range(4, 8):
                    x_stats(j)
                for b in range(3):
                    for t in range(2):
                        j = 4 * b + 4 + 2 * t
                        x_low(j)
                        x_low(j + 1)
                        if b == 2 and t == 1:
                            w_prep(1, 0)
                        h_mult(0, b, t)
                        for i in range(j + 4, min(j + 6, NT)):
                            x_stats(i)
                    if b < 2:
                        w_prep(0, 4 + b)
                        h_sums(0, b)
                    if b == 1:
                        w_sums(0)
                accumulate(0, 0, 0, DB // 2)
                w_prep(1, 1)
                accumulate(0, 0, DB // 2, DB)
                h_sums(0, 2)
                accumulate(0, 1, 0, DB // 2)
                w_prep(1, 2)
                h_mult(0, 3, 0)
                accumulate(0, 1, DB // 2, DB)
                w_prep(1, 3)
                h_mult(0, 3, 1)
                accumulate(0, 2, 0, DB)
                h_sums(0, 3)
                w_prep(1, 4)
                w_prep(1, 5)

            def group(g, next_tail=False):
                for b in range(NB):
                    before = (g - 1, NB - 1) if b == 0 else (g, b - 1)
                    early, late = (4, DB) if b == 0 else (4, 9)
                    h_mult(g, b, 0)
                    accumulate(*before, 0, early)
                    if b in (1, 2) or b == 3 and not next_tail:
                        w_prep(g + 1, 2 * b - 2, next_tail)
                    accumulate(*before, early, late)
                    h_mult(g, b, 1)
                    accumulate(*before, late, DB)
                    h_sums(g, b)
                    if b == 0:
                        w_sums(g)
                    elif b == 3 and next_tail:
                        tail_down_prep(4)
                    else:
                        w_prep(g + 1, 2 * b - 1, next_tail)

            def tail_group():
                for b in range(NB):
                    if b == 2:
                        roots()
                    if b == 0:
                        numerators()
                    tail_h_mult(b, 0)
                    if b == 0:
                        accumulate(NG - 1, NB - 1, 0, DB // 2)
                        tail_down_prep(5)
                    if b == 1:
                        resolvent()
                    if b == 3:
                        kernel_scale()
                    tail_h_mult(b, 1)
                    if b == 0:
                        accumulate(NG - 1, NB - 1, DB // 2, DB)
                        denominators()
                    if b == 2:
                        kernel_columns()
                    if b == 3:
                        dve.wait_ge(kt_done, 1)
                        dve.tensor_copy(krow, pg[0][0:M8, 0:P]).then_inc(krow_done, 1)
                    if b >= 1:
                        tail_accumulate(b - 1)
                    if b == 1:
                        cauchy_sums()

            first_group()
            dve.wait_ge(encoded, NB)
            with dve.Fori(0, (LOOP[1] - LOOP[0]) // 2) as it:
                for half_turn in range(2):
                    group(2 * it + (LOOP[0] + half_turn))
            group(NG - 1, next_tail=True)
            tail_group()
            for n in range(2):
                for c in range(2):
                    dve.wait_ge(shi_done, 2 * n + c + 1)
                    dve.scalar_tensor_tensor(out=strip[:, 1, n, c * SB:(c + 1) * SB], in0=(pg, pu)[n][c][:, :],
                                             scalar=ksc[:, 0:1].bitcast(f32), in1=strip[:, 0, n, c * SB:(c + 1) * SB],
                                             op0=ALU.mult, op1=ALU.subtract).then_inc(slo_done, 1)
            tail_accumulate(NB - 1)
            for d in range(2 * NT):
                part = acc[:, d // 2, (d % 2) * SB:(d % 2 + 1) * SB]
                dve.wait_ge(conv_done, d + 1)
                dve.scalar_tensor_tensor(out=part, in0=po[d % 4][:, :], scalar=ksc[:, 1:2].bitcast(f32), in1=part,
                                         op0=ALU.mult, op1=ALU.add).then_inc(conv_added, 1)


def _constants():
    l = np.arange(L)
    ang = np.pi * l / L
    angle = np.stack([np.cos(ang), np.sin(ang)])
    small = np.stack([np.cos(ang).reshape(P, M8), np.sin(ang).reshape(P, M8)], axis=1)
    a = np.arange(P)
    th = 2 * np.pi * np.outer(a, a) / P
    dft = np.stack([np.cos(th), np.sin(th)], axis=1)
    t = a[:, None, None] + P * np.arange(M8)[None, :, None]
    tw = 2 * np.pi * t * np.arange(M8)[None, None, :] / L
    twiddle = np.concatenate([np.cos(tw), -np.sin(tw)], axis=2) / L
    f = np.float32
    return {"ident": np.eye(P, dtype=f), "flip": np.eye(P, dtype=f)[::-1].copy(), "angle": angle.astype(f),
            "small": small.astype(f), "dft": dft.astype(f), "twiddle": twiddle.reshape(P, -1).astype(f)}


def _proj_words(wq):
    t = wq.T.reshape(4, P, I)
    main = t[:, :, :NG * CH].reshape(4, P, NG, P, 2).transpose(2, 1, 0, 4, 3).reshape(NG, P, 4 * CH)
    return main, t[:, :, NG * CH:].reshape(4, P, TAIL, 2)


def _proj_sz(scale, zero):
    t = np.stack([scale.T, zero.T]).reshape(2, 4, 4, I)
    main = t[..., :NG * CH].reshape(2, 4, 4, NG, P, 2).transpose(3, 2, 1, 0, 5, 4).reshape(NG, 4, 8 * CH)
    return main, t[..., NG * CH:].reshape(2, 4, 4, TAIL, 2).transpose(1, 2, 0, 3, 4)


def _tail_tiles(gate, up):
    (ga, gb), (ua, ub) = ((np.concatenate([a[..., 0], a[..., :TA, 1]], axis=-1), a[..., TA:, 1])
                          for a in (gate, up))
    return [np.moveaxis(part, 0, 1).reshape(gate.shape[1], -1)
            for part in (np.concatenate([ga, gb, ub], axis=-1), ua)]


def _down_words(wq):
    t = wq.T
    return t[:NG * P].reshape(NG, P, H), t[NG * P:]


def _down_sz(scale, zero):
    t = np.stack([scale.T, zero.T]).reshape(2, I // GROUP, 2, H // 2)
    main = t[:, :4 * NG].transpose(1, 2, 0, 3).reshape(NG, 4, 2 * H)
    return main, t[:, 4 * NG:].transpose(1, 0, 2, 3).reshape(-1, 2 * H)


def kernel(**inputs):
    import concourse.bacc as _bacc
    from concourse.bass_utils import run_bass_kernel_spmd as _run

    a = {k.replace("L0_attn_", "").replace("L0_ffn_", ""): np.asarray(v) for k, v in inputs.items()}
    rg, tg = _proj_words(a["gate_Wq"])
    ru, tu = _proj_words(a["up_Wq"])
    rd, td = _down_words(a["down_Wq"])
    zg, tzg = _proj_sz(a["gate_scale"], a["gate_zero"])
    zu, tzu = _proj_sz(a["up_scale"], a["up_zero"])
    zd, tzd = _down_sz(a["down_scale"], a["down_zero"])
    tg, tu = _tail_tiles(tg, tu)
    tzg, tzu = _tail_tiles(tzg, tzu)
    arrays = {"x": a["u"].reshape(S, H), "raw_gate": rg, "raw_up": ru, "raw_down": rd,
              "sz_gate": zg, "sz_up": zu, "sz_down": zd,
              "tail_gate": tg, "tail_up": tu, "tail_down": td,
              "tsz_gate": tzg, "tsz_up": tzu, "tsz_down": tzd,
              "lam": a["Lambda_ri"], "p": a["p_ri"], "q": a["q_ri"], "vc": a["Vc_ri"],
              "ct": a["Ct_ri"].reshape(NS, 2), "bp": a["Bp"], "d": a["D"], "ls": a["log_step"]}
    arrays.update(_constants())
    nc = _bacc.Bacc("TRN2", target_bir_lowering=False, num_devices=1, dynamic_dma_scratch_size=1024)
    feeds, args = {}, []
    for name, arr in arrays.items():
        arr = np.ascontiguousarray(arr)
        feeds[f"in_{name}"] = arr
        args.append(nc.dram_tensor(f"in_{name}", arr.shape, mybir.dt.from_np(arr.dtype), kind="ExternalInput").ap())
    out = nc.dram_tensor("out", (S, H), mybir.dt.float32, kind="ExternalOutput").ap()
    s4_plus_int4_swiglu(nc, *args, out)
    r = _run(nc, [feeds], core_ids=[0])
    return r.results[0]["out"].reshape(1, S, H)
```
